# Optimizing a Trainium2 kernel written in Bass

```python
import numpy as np
import jax
import jax.numpy as jnp

def _softmax(x, axis=-1):
    return jax.nn.softmax(x, axis=axis)

def _gelu(x):
    return jax.nn.gelu(x, approximate=True)

def _silu(x):
    return jax.nn.silu(x)

def _sigmoid(x):
    return jax.nn.sigmoid(x)

def _layernorm(x, axis=-1, eps=1e-05):
    m = jnp.mean(x, axis=axis, keepdims=True)
    v = jnp.var(x, axis=axis, keepdims=True)
    return (x - m) / jnp.sqrt(v + eps)

def _scatter_add(tgt, idx, src, axis=0):
    return tgt.at[idx].add(src)

def _segment_sum(src, seg, n):
    return jax.ops.segment_sum(src, seg, n)
kernel_name = 'mk_flamingo_gated_d1_seqx_r2_e57c05'

def setup_inputs(seed: int=0):
    np.random.seed(seed)
    _w = jnp.asarray

    def _rec_inputs():
        import jax
        import jax.numpy as jnp
        _rk = jax.random.key(seed)
        x = 7.22e-05 + 1 * jax.random.normal(jax.random.fold_in(_rk, 1), (8, 100, 512), jnp.float32)
        _lenS = 100 - jax.random.randint(jax.random.fold_in(_rk, 7), (8,), 0, max(1, 100 // 4) + 1, jnp.int32)
        _lenS2 = 722 - jax.random.randint(jax.random.fold_in(_rk, 8), (8,), 0, max(1, 722 // 4) + 1, jnp.int32)
        _ctx_1024P = jax.random.normal(jax.random.fold_in(_rk, 11), (8, 16, 512), jnp.float32)
        _ctx_1024c = jax.random.dirichlet(jax.random.fold_in(_rk, 511), 0.3 * jnp.ones((16,), jnp.float32), (8, 722))
        _ctx_1024t = jnp.einsum('bsk,bkd->bsd', _ctx_1024c, _ctx_1024P)
        _ctx_1024t = _ctx_1024t * jax.lax.rsqrt(jnp.mean(jnp.square(_ctx_1024t)) + 1e-12) * 0.953939
        ctx_1024 = 4.13588e-05 + 0.999923 * (_ctx_1024t + 0.3 * jax.random.normal(jax.random.fold_in(_rk, 611), (8, 722, 512), jnp.float32))
        _validS = jnp.arange(100)[None, :] < _lenS[:, None]
        _validS2 = jnp.arange(722)[None, :] < _lenS2[:, None]
        _causal = jnp.tril(jnp.ones((100, 100), dtype=bool))
        mask_BxS2_bk0 = jnp.logical_not(jnp.broadcast_to(_validS2[:, :], (8, 722)))
        _g = jax.random.normal(jax.random.fold_in(_rk, 9001), (2, 1), jnp.float32)
        _g = jnp.sign(_g) * jnp.maximum(jnp.abs(_g), 1.0) + (_g == 0) * 1.0
        g_xattn = _g[0]
        g_ffn = _g[1]
        return (x, ctx_1024, mask_BxS2_bk0, g_xattn, g_ffn)
    x, ctx_1024, mask_BxS2_bk0, g_xattn, g_ffn = _rec_inputs()

    def _L0_xattn_setup():
        import math
        import jax, jax.numpy as jnp
        import numpy as np
        HIDDEN = 512
        NUM_HEADS = 16
        HEAD_DIM = HIDDEN // NUM_HEADS
        B, S = (4, 1024)

        def _layer_norm_scores(x, eps=1e-08):
            mean = jnp.mean(x, axis=-1, keepdims=True)
            sigma = jnp.std(x, axis=-1, keepdims=True, ddof=1)
            return (x - mean) / (sigma + eps)
        key = jax.random.key(seed)
        ks = jax.random.split(key, 10)
        sc_in = 1.0 / math.sqrt(HIDDEN)
        inp = {'query': jax.random.normal(ks[0], (B, S, HIDDEN), jnp.float32), 'key': jax.random.normal(ks[1], (B, S, HIDDEN), jnp.float32), 'value': jax.random.normal(ks[2], (B, S, HIDDEN), jnp.float32), 'mask': jax.random.randint(ks[3], (B, S), 0, 2).astype(bool), 'Wq': jax.random.normal(ks[4], (HIDDEN, HEAD_DIM), jnp.float32) * sc_in, 'bq': jnp.zeros((HEAD_DIM,), jnp.float32), 'Wk': jax.random.normal(ks[5], (HIDDEN, HEAD_DIM), jnp.float32) * sc_in, 'bk': jnp.zeros((HEAD_DIM,), jnp.float32), 'Wv': jax.random.normal(ks[6], (HIDDEN, HEAD_DIM), jnp.float32) * sc_in, 'bv': jnp.zeros((HEAD_DIM,), jnp.float32), 'Wout': jax.random.normal(ks[7], (HIDDEN, HIDDEN), jnp.float32) * sc_in, 'bout': jnp.zeros((HIDDEN,), jnp.float32), 'seq_mask': 0}
        return inp
    _L0_xattn_all = _L0_xattn_setup()
    _L0_xattn_in = {k: v for k, v in _L0_xattn_all.items() if k in ('Wq', 'bq', 'Wk', 'bk', 'Wv', 'bv', 'Wout', 'bout')}
    del _L0_xattn_all

    def _L0_ffn_setup():
        import jax, jax.numpy as jnp
        import numpy as np
        E, H, I, K = (8, 512, 1024, 2)
        B, S = (4, 1024)
        key = jax.random.key(seed)
        k1, k2, k3, k4 = jax.random.split(key, 4)
        x = jax.random.normal(k1, (B, S, H), dtype=jnp.float32)
        router_w = jax.random.uniform(k2, (E, H), dtype=jnp.float32, minval=-1.0, maxval=1.0) / np.sqrt(H).astype(np.float32)
        w13 = jax.random.normal(k3, (E, H, 2 * I), dtype=jnp.float32) * 0.02
        w2 = jax.random.normal(k4, (E, I, H), dtype=jnp.float32) * 0.02
        return {'x': x, 'router_w': router_w, 'w13': w13, 'w2': w2}
    _L0_ffn_all = _L0_ffn_setup()
    _L0_ffn_in = {k: v for k, v in _L0_ffn_all.items() if k in ('router_w', 'w13', 'w2')}
    del _L0_ffn_all
    return {'x': x, 'ctx_1024': ctx_1024, 'mask_BxS2_bk0': mask_BxS2_bk0, 'g_xattn': g_xattn, 'g_ffn': g_ffn, 'L0_xattn_Wq': _L0_xattn_in['Wq'], 'L0_xattn_bq': _L0_xattn_in['bq'], 'L0_xattn_Wk': _L0_xattn_in['Wk'], 'L0_xattn_bk': _L0_xattn_in['bk'], 'L0_xattn_Wv': _L0_xattn_in['Wv'], 'L0_xattn_bv': _L0_xattn_in['bv'], 'L0_xattn_Wout': _L0_xattn_in['Wout'], 'L0_xattn_bout': _L0_xattn_in['bout'], 'L0_ffn_router_w': _L0_ffn_in['router_w'], 'L0_ffn_w13': _L0_ffn_in['w13'], 'L0_ffn_w2': _L0_ffn_in['w2']}

def reference(x, ctx_1024, mask_BxS2_bk0, g_xattn, g_ffn, L0_xattn_Wq, L0_xattn_bq, L0_xattn_Wk, L0_xattn_bk, L0_xattn_Wv, L0_xattn_bv, L0_xattn_Wout, L0_xattn_bout, L0_ffn_router_w, L0_ffn_w13, L0_ffn_w2):
    import jax
    import jax.numpy as jnp

    def _L0_xattn_ref(query, key, value, mask, Wq, bq, Wk, bk, Wv, bv, Wout, bout, seq_mask):
        import math
        import jax, jax.numpy as jnp
        import numpy as np
        HIDDEN = 512
        NUM_HEADS = 16
        HEAD_DIM = HIDDEN // NUM_HEADS
        B, S = (4, 1024)

        def _layer_norm_scores(x, eps=1e-08):
            mean = jnp.mean(x, axis=-1, keepdims=True)
            sigma = jnp.std(x, axis=-1, keepdims=True, ddof=1)
            return (x - mean) / (sigma + eps)
        q = query @ Wq + bq
        k = key @ Wk + bk
        v = value @ Wv + bv
        scores = jnp.einsum('bqd,bkd->bqk', q, k) / math.sqrt(HIDDEN)
        scores = _layer_norm_scores(scores)
        m = jnp.broadcast_to(mask[:, None, :], scores.shape)
        if seq_mask:
            tri = jnp.triu(jnp.ones(scores.shape[-2:], bool), k=1)
            m = m | tri[None]
        scores = scores + jnp.where(m, jnp.float32(-1e-32), jnp.float32(0.0))
        attn = jax.nn.softmax(scores, axis=-1)
        head = jnp.einsum('bqk,bkd->bqd', attn, v)
        attention = jnp.tile(head, (1, 1, NUM_HEADS))
        return attention @ Wout + bout

    def _L0_ffn_ref(x, router_w, w13, w2):
        import jax, jax.numpy as jnp
        import numpy as np
        E, H, I, K = (8, 512, 1024, 2)
        B, S = (4, 1024)
        logits = jnp.einsum('bsh,eh->bse', x, router_w)
        probs = jax.nn.softmax(logits, axis=-1)
        weights, indices = jax.lax.top_k(probs, K)
        weights = weights / (weights.sum(axis=-1, keepdims=True) + 1e-06)
        h13 = jnp.einsum('bsh,ehi->bsei', x, w13)
        gate, up = jnp.split(h13, 2, axis=-1)
        h = jax.nn.silu(gate) * up
        y = jnp.einsum('bsei,eih->bseh', h, w2)
        y_sel = jnp.take_along_axis(y, indices[..., None], axis=2)
        return (y_sel * weights[..., None]).sum(axis=2)
    x = x + jnp.tanh(g_xattn[0]) * _L0_xattn_ref(_layernorm(x, axis=-1), ctx_1024, ctx_1024, mask_BxS2_bk0, L0_xattn_Wq, L0_xattn_bq, L0_xattn_Wk, L0_xattn_bk, L0_xattn_Wv, L0_xattn_bv, L0_xattn_Wout, L0_xattn_bout, 0)
    x = x + jnp.tanh(g_ffn[0]) * _L0_ffn_ref(_layernorm(x, axis=-1), L0_ffn_router_w, L0_ffn_w13, L0_ffn_w2)
    return x

_drawn_inputs = setup_inputs


def setup_inputs(seed=0):
    import zlib

    import numpy as np

    out = dict(_drawn_inputs(seed))
    spreads = {'L0_xattn_bq': (0.0, 0.489),
     'L0_xattn_bk': (0.0, 0.8),
     'L0_xattn_bv': (0.0, 0.1),
     'L0_xattn_bout': (0.0, 0.1)}
    factors = {}
    for name, (base, spread) in spreads.items():
        noise = np.random.default_rng([zlib.crc32(name.encode()), seed]).standard_normal(out[name].shape)
        drawn = base * np.exp(spread * noise) if base else spread * noise
        out[name] = jnp.asarray(drawn.astype(out[name].dtype))
    for name, factor in factors.items():
        out[name] = (out[name] * factor).astype(out[name].dtype)
    return out
```

```python
from contextlib import ExitStack

import concourse.bass as bass
from concourse import mybir

ALU = mybir.AluOpType
ACT = mybir.ActivationFunctionType
F32 = mybir.dt.float32
F32R = mybir.dt.float32r
I32 = mybir.dt.int32
U32 = mybir.dt.uint32
U8 = mybir.dt.uint8
AX = mybir.AxisListType

P = 128
MASK_TERM = -1e-32
SIGMA_EPS = 1e-8
LN_EPS = 1e-5
TOPK_EPS = 1e-6


def gated_block(nc, x, ctx_in, mask, g_xattn, g_ffn, Wq, bq, Wk, bk, Wv, bv, Wout, bout,
                router_w, w13, w2, out):
    NB, SQ, H = x.shape
    SK = ctx_in.shape[1]
    D = Wq.shape[1]
    E, _, I2 = w13.shape
    I = I2 // 2
    HC = H // P
    IC = I // P
    T = NB * SQ
    KT = -(-SK // P)
    KL = SK - (KT - 1) * P
    REP = H // D
    CAP = -(-T // P) * P
    ROWS = E * CAP + P
    TILES = 2 * T // P + E + 1
    NQ = 4
    QW = I // NQ
    QC = QW // P
    NO_TOKEN = 1 << 12
    assert NQ * 2 * QW * 4 <= 8192 and 2 * D == 64 and P % D == 0

    mask = mask.bitcast(U8).rearrange("(b k) -> b k", b=NB)

    es = ExitStack()
    with es:
        def sem(name):
            return es.enter_context(nc.semaphore(name))

        def sb(stack, name, shape, dt=F32):
            return stack.enter_context(nc.sbuf_tensor(name, shape, dt))

        xn2_d = nc.dram_tensor("xn2_d", [T, H], F32).ap()
        lists_d = nc.dram_tensor("lists_d", [ROWS, 2], I32).ap()
        out_rows = out.rearrange("b s d -> (b s) d")

        turnA = es.enter_context(nc.psum_tensor("turnA", [P, 1024], F32))
        turnB = es.enter_context(nc.psum_tensor("turnB", [P, 1024], F32))
        kvp = es.enter_context(nc.psum_tensor("kvp", [P, 1024], F32))
        scp = es.enter_context(nc.psum_tensor("scp", [P, 1024], F32))

        ident = sb(es, "ident", [P, P])
        ones = sb(es, "ones", [P, P])
        stage13 = sb(es, "stage13", [P, HC, I2])
        stage2 = sb(es, "stage2", [P, IC, H])
        w13h = sb(es, "w13h", [P, HC, I2], F32R)
        w13l = sb(es, "w13l", [P, HC, I2], F32R)
        first_tile = sb(es, "first_tile", [1, E + 1], I32)
        tile_row = sb(es, "tile_row", [1, TILES], I32)

        a = ExitStack()
        ctx_t = [sb(a, f"ctx_t{i}", [P, KT, H]) for i in range(2)]
        x_t = [sb(a, f"x_t{i}", [SQ, H]) for i in range(2)]
        mask_u = [sb(a, f"mask_u{i}", [SQ, SK], U8) for i in range(2)]
        mterm = [sb(a, f"mterm{i}", [SQ, SK]) for i in range(2)]
        ctxTh = [sb(a, f"ctxTh{i}", [P, SK], F32R) for i in range(2)]
        ctxTl = [sb(a, f"ctxTl{i}", [P, SK], F32R) for i in range(2)]
        kv = sb(a, "kv", [P, SK])
        z = sb(a, "z", [SQ, SK])
        prob = sb(a, "prob", [SQ, SK])
        probT = sb(a, "probT", [P, KT, SQ])
        vn = [sb(a, f"vn{i}", [P, KT, 2 * D]) for i in range(2)]
        xn = sb(a, "xn", [SQ, H])
        xnT = sb(a, "xnT", [P, HC, SQ])
        qT = sb(a, "qT", [2 * D, SQ])
        headT = sb(a, "headT", [2 * D, SQ])
        xc = [sb(a, f"xc{i}", [SQ, H]) for i in range(3)]
        x2 = [sb(a, f"x2{i}", [SQ, H]) for i in range(2)]
        xn2 = [sb(a, f"xn2{i}", [SQ, H]) for i in range(2)]
        xn2T = sb(a, "xn2T", [P, HC, SQ])
        wq2 = sb(a, "wq2", [P, HC, 2 * D])
        wkv_raw = sb(a, "wkv_raw", [P, 2, HC, D])
        wkv = sb(a, "wkv", [P, HC, P], F32R)
        wsum = sb(a, "wsum", [2 * D, H])
        sel = sb(a, "sel", [P, 2 * D])
        rw_rows = xc[1][0:E, :]
        rwT = sb(a, "rwT", [P, HC, E])
        bout_r = xc[2][0:1, :]
        bv_c = sb(a, "bv_c", [D, 1])
        bv_b = sb(a, "bv_b", [D, SQ])
        bq_c = sb(a, "bq_c", [2 * D, 1])
        kvb = sb(a, "kvb", [P, 1])
        g_in = sb(a, "g_in", [P, 2])
        g_t = sb(a, "g_t", [P, 2])
        crow = sb(a, "crow", [SQ, H])
        tri = sb(a, "tri", [SQ, SQ])
        before8 = sb(a, "before8", [E, E + 1])
        tok = sb(a, "tok", [SQ, NB], I32)
        e_int = sb(a, "e_int", [SQ, E], I32)
        e_num = sb(a, "e_num", [SQ, E])
        e_base = sb(a, "e_base", [1, E])
        t_int = sb(a, "t_int", [E, TILES], I32)
        t_num = sb(a, "t_num", [E, TILES])
        empty = sb(a, "empty", [P, ROWS // P, 2], I32)
        half = sb(a, "half", [SQ, 3])
        bn1 = sb(a, "bn1", [SQ, 6])
        ln1 = sb(a, "ln1", [SQ, 2])
        rs1 = sb(a, "rs1", [SQ, 2])
        bns = sb(a, "bns", [SQ, 2, 6])
        lns = sb(a, "lns", [SQ, 2])
        sig = sb(a, "sig", [SQ, 6])
        zmax = sb(a, "zmax", [SQ, 2])
        psum_p = sb(a, "psum_p", [SQ, 1])
        gs = sb(a, "gs", [SQ, 2])
        bn2 = sb(a, "bn2", [SQ, 6])
        ln2 = [sb(a, f"ln2{i}", [SQ, 2]) for i in range(2)]
        rs2 = sb(a, "rs2", [SQ, 2])
        ltop = sb(a, "ltop", [SQ, 8])
        nlmax = sb(a, "nlmax", [SQ, 1])
        pe_e = sb(a, "pe_e", [SQ, E])
        pe_s = sb(a, "pe_s", [SQ, 2])
        pr = sb(a, "pr", [SQ, E])
        ptop = sb(a, "ptop", [SQ, 8])
        pidx = sb(a, "pidx", [SQ, 8], U32)
        idxf = sb(a, "idxf", [SQ, 2])
        hot = [sb(a, f"hot{i}", [SQ, 2, E]) for i in range(2)]
        both = [sb(a, f"both{i}", [SQ, E]) for i in range(2)]
        taken = sb(a, "taken", [SQ, NB + 1, E])
        wgt = [sb(a, f"wgt{i}", [SQ, 4]) for i in range(2)]
        hr = sb(a, "hr", [SQ, 2, E])
        place_f = sb(a, "place_f", [SQ, 2])
        place = sb(a, "place", [SQ, NB, 2], I32)
        entry = sb(a, "entry", [SQ, NB, 2, 2], I32)
        cnt_i = sb(a, "cnt_i", [E, 2], I32)
        nt = sb(a, "nt", [E, 3])
        past = sb(a, "past", [E, TILES])
        ncum = sb(a, "ncum", [E, 1])
        a.close()

        w2h = sb(es, "w2h", [P, IC, H], F32R)
        w2l = sb(es, "w2l", [P, IC, H], F32R)
        xg = sb(es, "xg", [P, H])
        xTh = sb(es, "xTh", [P, HC, P], F32R)
        xTl = sb(es, "xTl", [P, HC, P], F32R)
        sg = [sb(es, f"sg{i}", [P, QW]) for i in range(2)]
        h_t = sb(es, "h_t", [P, NQ, QW])
        hTh = sb(es, "hTh", [P, NQ, QC * P], F32R)
        hTl = sb(es, "hTl", [P, NQ, QC * P], F32R)
        yw = sb(es, "yw", [P, H])
        ent_next = sb(es, "ent_next", [P, 2], I32)
        ent = sb(es, "ent", [P, 2], I32)
        gidx = sb(es, "gidx", [P, 1], I32)

        names = """x_in0 x_in1 ctx_in0 ctx_in1 wout_in wq_in wkv_in small_in rw_in lists_set lists_put0 lists_put1
        out_put0 out_put1 xn2_put0 xn2_put1
        ident_zero ident_made ones_made consts_made iotas_made consts_copied taken_zero kvb_zero
        sel_made wsum_done wsum_copied wkv_hi wkv_lo rw_turned rw_copied tanh_done bv_spread crow_done crow_made bq_scaled
        ln1_stat ln1_aggr rstd1_a rstd1 xn_ready xc_ready mterm_ready
        xn_turned xnT_copied q_done q_copied ctx_turned ctx_hi ctx_lo proj_done kv_done kv_copied
        v_turned v_copied scores_done sstat0 s_aggr sig_step sig_ready z_done z_masked negmax exp_done rsum
        gsum prob_turned probT_copied head_done head_copied out_done x2_ready ln2_stat ln2_aggr rstd2_a rstd2
        xn2_ready xn2_turned xn2T_copied logits_done lmax_done nlmax_done lexp_done lrec probs_done ptop_done pidx_done
        pool_w pool_held idx_copied hot_made both_made taken_made weight_made rank_done hr_done placef_done place_made
        cnt_done cnt_int cnt_shift nt_f nt_ready cum_done ncum_copied past_made tilerow_done tiles_ready first_ready
        attn_done""".split()
        S = {n: sem(n) for n in names}
        names2 = """st13_0 st13_1 st13_2 st13_3 st2_0 st2_1
        w_hi w_lo gu_done silu_done h_done ht_done hh_done hl_done y_done y_ready
        list_in gidx_made gathered yw_free ent_copied y_added xg_turned xh_done xl_done""".split()
        S.update({n: sem(n) for n in names2})

        block = es.enter_context(nc.Block())
        ROUNDS = range(-1, NB + 4)

        def live(b):
            return 0 <= b < NB

        n_small = 10

        @block.sync
        def _(sp):
            sp.dma_start(x_t[0][:], x[0]).then_inc(S["x_in0"], 16)
            sp.dma_start(mask_u[0][:], mask[0:1, :].partition_broadcast(SQ)).then_inc(S["x_in0"], 16)
            sp.dma_start(ctx_t[1][:, 0:HC, :], Wout.rearrange("(c p) n -> p c n", p=P)).then_inc(S["wout_in"], 16)
            sp.dma_start(wkv_raw[:, 0], Wk.rearrange("(c p) n -> p c n", p=P)).then_inc(S["wkv_in"], 16)
            sp.dma_start(wkv_raw[:, 1], Wv.rearrange("(c p) n -> p c n", p=P)).then_inc(S["wkv_in"], 16)
            for r in range(2):
                sp.dma_start(wq2[:, :, r * D:(r + 1) * D], Wq.rearrange("(c p) n -> p c n", p=P)).then_inc(S["wq_in"], 16)

            def load_ctx(b):
                s = S[f"ctx_in{b % 2}"]
                sp.dma_start(ctx_t[b % 2][:, 0:KT - 1, :],
                             ctx_in[b, 0:(KT - 1) * P, :].rearrange("(k p) d -> p k d", p=P)).then_inc(s, 16)
                sp.dma_start(ctx_t[b % 2][0:KL, KT - 1, :], ctx_in[b, (KT - 1) * P:SK, :]).then_inc(s, 16)

            load_ctx(0)
            sp.dma_start(rw_rows, router_w).then_inc(S["rw_in"], 16)
            sp.wait_ge(S["kvb_zero"], 1)
            sp.dma_start(kvb[0:D, :], bk.rearrange("(d o) -> d o", o=1)).then_inc(S["small_in"], 16)
            sp.dma_start(bv_c[:], bv.rearrange("(d o) -> d o", o=1)).then_inc(S["small_in"], 16)
            for r in range(2):
                sp.dma_start(bq_c[r * D:(r + 1) * D, :], bq.rearrange("(d o) -> d o", o=1)).then_inc(S["small_in"], 16)
            sp.dma_start(bout_r, bout.rearrange("(o d) -> o d", o=1)).then_inc(S["small_in"], 16)
            sp.dma_start(g_in[:, 0:1], g_xattn.rearrange("(o d) -> o d", o=1).partition_broadcast(P)).then_inc(S["small_in"], 16)
            sp.dma_start(g_in[:, 1:2], g_ffn.rearrange("(o d) -> o d", o=1).partition_broadcast(P)).then_inc(S["small_in"], 16)
            for b in range(1, NB):
                s = S[f"x_in{b % 2}"]
                if b >= 2:
                    sp.wait_ge(S["xn_ready"], b - 1)
                    sp.wait_ge(S["xc_ready"], b - 1)
                    sp.wait_ge(S["mterm_ready"], b - 1)
                sp.dma_start(x_t[b % 2][:], x[b]).then_inc(s, 16)
                sp.dma_start(mask_u[b % 2][:], mask[b:b + 1, :].partition_broadcast(SQ)).then_inc(s, 16)
                if b == 1:
                    sp.wait_ge(S["wsum_done"], 1)
                else:
                    sp.wait_ge(S["ctx_turned"], HC * (b - 1))
                load_ctx(b)
                if b == 2:
                    sp.wait_ge(S["consts_copied"], 1)
                    sp.dma_start(lists_d.rearrange("(p r) t -> p r t", p=P), empty[:]).then_inc(S["lists_set"], 16)

            def load_w13(e, c):
                sp.dma_start(stage13[:, c, :], w13[e, c * P:(c + 1) * P, :]).then_inc(S[f"st13_{c}"], 16)

            def load_w2(e, u):
                half_ic = IC // 2
                sp.dma_start(stage2[:, u * half_ic:(u + 1) * half_ic, :],
                             w2[e, u * half_ic * P:(u + 1) * half_ic * P, :].rearrange("(c p) n -> p c n", p=P)
                             ).then_inc(S[f"st2_{u}"], 16)

            for c in range(HC):
                load_w13(0, c)
            for u in range(2):
                load_w2(0, u)
            with sp.Fori(1, E) as e:
                sp.wait_ge(S["w_lo"], e * 6 - 2)
                for c in range(HC):
                    sp.dma_start(stage13[:, c, :], w13[bass.ds(e, 1), c * P:(c + 1) * P, :].rearrange("o p n -> p (o n)")
                                 ).then_inc(S[f"st13_{c}"], 16)
                for u in range(2):
                    sp.wait_ge(S["w_lo"], e * 6 - 1 + u)
                    hic = IC // 2
                    sp.dma_start(stage2[:, u * hic:(u + 1) * hic, :],
                                 w2[bass.ds(e, 1), u * hic * P:(u + 1) * hic * P, :].rearrange("o (c p) n -> p (o c) n", p=P)
                                 ).then_inc(S[f"st2_{u}"], 16)

        @block.tensor
        def _(pe):
            pe.wait_ge(S["ident_made"], 1)
            pe.wait_ge(S["ones_made"], 1)
            pe.wait_ge(S["wout_in"], 16)
            pe.wait_ge(S["sel_made"], 2)
            for c in range(HC):
                mm = pe.matmul(kvp[0:2 * D, 0:H], sel[:], ctx_t[1][:, c, :], start=(c == 0), stop=(c == HC - 1))
            mm.then_inc(S["wsum_done"], 1)
            pe.wait_ge(S["rw_in"], 16)
            for c in range(HC):
                mm = pe.transpose(kvp[:, 512 + E * c:512 + E * (c + 1)], rw_rows[:, c * P:(c + 1) * P], ident[0:E, 0:E])
            mm.then_inc(S["rw_turned"], 1)
            pe.wait_ge(S["wsum_copied"], 1)
            pe.wait_ge(S["bv_spread"], 1)
            pe.wait_ge(S["small_in"], 16 * 7)
            pe.matmul(scp[0:SQ, 0:H], bv_b[:], wsum[0:D, :], start=True, stop=False)
            pe.matmul(scp[0:SQ, 0:H], ones[0:1, 0:SQ], bout_r, start=False, stop=True).then_inc(S["crow_done"], 1)
            pe.wait_ge(S["rw_copied"], 1)

            def turn_ctx(b, c):
                region = turnB if c % 2 == 0 else turnA
                for k in range(KT):
                    n = P if k < KT - 1 else KL
                    mm = pe.transpose(region[:, k * P:k * P + n], ctx_t[b % 2][0:n, k, c * P:(c + 1) * P], ident[0:n, 0:n])
                mm.then_inc(S["ctx_turned"], 1)

            def project(b, c):
                n = HC * b + c
                pe.wait_ge(S["ctx_lo"], n + 1)
                for i, part in enumerate((ctxTh[n % 2], ctxTl[n % 2])):
                    for k0, k1 in ((0, 512), (512, SK)):
                        mm = pe.matmul(kvp[:, k0:k1], wkv[:, c, :], part[:, k0:k1], start=(c == 0 and i == 0),
                                       stop=(c == HC - 1 and i == 1))
                mm.then_inc(S["proj_done"], 1)

            for i in ROUNDS:
                if live(i):
                    pe.wait_ge(S["xn_ready"], i + 1)
                    if i >= 2:
                        pe.wait_ge(S["x2_ready"], i - 1)
                    elif i == 1:
                        pe.wait_ge(S["v_copied"], 2)
                    for c in range(HC):
                        mm = pe.transpose(turnA[:, c * SQ:(c + 1) * SQ], xn[:, c * P:(c + 1) * P], ident[0:SQ, 0:SQ])
                    mm.then_inc(S["xn_turned"], 1)
                    pe.wait_ge(S[f"ctx_in{i % 2}"], 32 * (i // 2 + 1))
                    if i >= 1:
                        pe.wait_ge(S["ctx_lo"], HC * i)
                    if i >= 3:
                        pe.wait_ge(S["xn2T_copied"], i - 2)
                    turn_ctx(i, 0)
                    pe.wait_ge(S["xnT_copied"], i + 1)
                    if i == 0:
                        pe.wait_ge(S["wq_in"], 32)
                        pe.wait_ge(S["wkv_lo"], 2)
                    if i >= 1:
                        pe.wait_ge(S["kv_copied"], i)
                    if i >= 2:
                        pe.wait_ge(S["head_copied"], i - 1)
                    for c in range(HC):
                        mm = pe.matmul(kvp[0:2 * D, P:P + SQ], wq2[:, c, :], xnT[:, c, :], start=(c == 0), stop=(c == HC - 1))
                    mm.then_inc(S["q_done"], 1)
                    turn_ctx(i, 1)
                    pe.wait_ge(S["q_copied"], i + 1)
                    if i >= 3:
                        pe.wait_ge(S["lexp_done"], i - 2)
                        pe.wait_ge(S["lmax_done"], i - 2)
                    if i >= 4:
                        pe.wait_ge(S["hr_done"], 2 * (i - 3))
                    project(i, 0)
                    turn_ctx(i, 2)
                    project(i, 1)
                    turn_ctx(i, 3)
                    project(i, 2)
                if live(i - 1):
                    b = i - 1
                    if live(i):
                        pe.wait_ge(S["ctx_lo"], HC * i + 3)
                    else:
                        pe.wait_ge(S["xn2T_copied"], i - 2)
                    pe.wait_ge(S["exp_done"], b + 1)
                    for k in range(KT):
                        n = P if k < KT - 1 else KL
                        mm = pe.transpose(turnB[0:n, (k // 5) * 512 + (k % 5) * SQ:(k // 5) * 512 + (k % 5) * SQ + SQ],
                                          prob[:, k * P:k * P + n], ident[0:SQ, 0:SQ])
                    mm.then_inc(S["prob_turned"], 1)
                if live(i):
                    project(i, 3)
                    pe.wait_ge(S["kv_copied"], i + 1)
                    for k in range(KT):
                        n = P if k < KT - 1 else KL
                        mm = pe.transpose(turnA[0:n, k * 2 * D:(k + 1) * 2 * D], kv[2 * D:4 * D, k * P:k * P + n],
                                          ident[2 * D:4 * D, 2 * D:4 * D])
                    mm.then_inc(S["v_turned"], 1)
                    if i == 0:
                        pe.wait_ge(S["crow_made"], 1)
                    if i >= 1:
                        pe.wait_ge(S["z_done"], i)
                    for k0, k1 in ((0, 512), (512, SK)):
                        mm = pe.matmul(scp[0:SQ, k0:k1], qT[:], kv[0:2 * D, k0:k1], start=True, stop=True)
                    mm.then_inc(S["scores_done"], 1)
                if live(i - 1):
                    b = i - 1
                    pe.wait_ge(S["probT_copied"], 2 * (b + 1))
                    pe.wait_ge(S["v_copied"], 2 * (b + 1))
                    for k in range(KT):
                        n = P if k < KT - 1 else KL
                        mm = pe.matmul(kvp[0:2 * D, 0:SQ], vn[b % 2][0:n, k, :], probT[0:n, k, :], start=(k == 0), stop=(k == KT - 1))
                    mm.then_inc(S["head_done"], 1)
                if live(i - 2):
                    b = i - 2
                    if live(i - 1):
                        pe.wait_ge(S["probT_copied"], 2 * i)
                    pe.wait_ge(S["xn2_ready"], b + 1)
                    for c in range(HC):
                        mm = pe.transpose(turnB[:, c * SQ:(c + 1) * SQ], xn2[b % 2][:, c * P:(c + 1) * P], ident[0:SQ, 0:SQ])
                    mm.then_inc(S["xn2_turned"], 1)
                if live(i - 3):
                    b = i - 3
                    pe.wait_ge(S["taken_made"], b + 1)
                    if b >= 1:
                        pe.wait_ge(S["hr_done"], 2 * b)
                        pe.wait_ge(S["lexp_done"], b + 1)
                    pe.matmul(kvp[0:SQ, 784:784 + E], tri[:], both[b % 2][:], start=True, stop=False)
                    pe.matmul(kvp[0:SQ, 784:784 + E], ones[0:SQ, 0:SQ], taken[:, b, :], start=False, stop=False)
                    pe.matmul(kvp[0:SQ, 784:784 + E], ones[0:1, 0:SQ], e_base[:], start=False, stop=True).then_inc(S["rank_done"], 1)
                if live(i - 1):
                    b = i - 1
                    pe.wait_ge(S["head_copied"], b + 1)
                    if live(i):
                        pe.wait_ge(S["v_copied"], 2 * (i + 1))
                    pe.matmul(turnA[0:SQ, 0:H], headT[:], wsum[:], start=True, stop=True).then_inc(S["out_done"], 1)
                if live(i - 2):
                    b = i - 2
                    pe.wait_ge(S["xn2T_copied"], b + 1)
                    if live(i - 3):
                        pe.wait_ge(S["hr_done"], 2 * (i - 2))
                    for c in range(HC):
                        mm = pe.matmul(kvp[0:SQ, 768:768 + E], xn2T[:, c, :], rwT[:, c, :], start=(c == 0), stop=(c == HC - 1))
                    mm.then_inc(S["logits_done"], 1)

            pe.wait_ge(S["hr_done"], 2 * NB)
            pe.matmul(kvp[0:E, 800:801], taken[:, NB, :], ones[0:SQ, 0:1], start=True, stop=True).then_inc(S["cnt_done"], 1)
            pe.wait_ge(S["nt_ready"], 1)
            pe.matmul(scp[0:E, 0:1], before8[:, 1:E + 1], nt[:, 1:2], start=True, stop=True)
            pe.matmul(scp[0:1, 512:512 + E + 1], nt[:, 1:2], before8[:], start=True, stop=True).then_inc(S["cum_done"], 1)
            pe.wait_ge(S["past_made"], 1)
            pe.wait_ge(S["first_ready"], 1)
            pe.matmul(scp[0:1, 0:TILES], ones[0:E - 1, 0:1], past[0:E - 1, :], start=True, stop=True).then_inc(S["tilerow_done"], 1)
            pe.drain().then_inc(S["attn_done"], 1)

            def turn_x(t):
                pe.wait_ge(S["gathered"], 16 * t + 16)
                for c in range(HC):
                    mm = pe.transpose(scp[:, c * P:(c + 1) * P], xg[:, c * P:(c + 1) * P], ident[:])
                mm.then_inc(S["xg_turned"], 1)

            def gate_up(t, q, e):
                if q == 0:
                    pe.wait_ge(S["xl_done"], t + 1)
                if e is not None:
                    pe.wait_ge(S["w_lo"], 6 * e + q + 1)
                pe.wait_ge(S["h_done"], NQ * t + q + 1)
                region = (turnA, turnB)[q // 2][:, (q % 2) * 512:(q % 2) * 512 + 2 * QW]
                terms = ((xTh, w13h), (xTl, w13h), (xTh, w13l))
                for c in range(HC):
                    for i, (xp, wp) in enumerate(terms):
                        rhs = wp[:, c, :].rearrange("p (g n) -> p g n", g=2)[:, :, q * QW:(q + 1) * QW]
                        mm = pe.matmul(region, xp[:, c, :], rhs, start=(c == 0 and i == 0), stop=(c == HC - 1 and i == 2))
                mm.then_inc(S["gu_done"], 1)

            def turn_h(t, q):
                pe.wait_ge(S["h_done"], NQ * t + NQ + q + 1)
                pe.wait_ge(S["hl_done"], NQ * t + q + 3)
                for j in range(QC):
                    mm = pe.transpose(kvp[:, (q % 2) * 512 + j * P:(q % 2) * 512 + (j + 1) * P],
                                      h_t[:, q, j * P:(j + 1) * P], ident[:])
                mm.then_inc(S["ht_done"], 1)

            def down(t, q, e):
                if q == 0:
                    pe.wait_ge(S["y_ready"], t + 1)
                if e is not None and q % 2 == 0:
                    pe.wait_ge(S["w_lo"], 6 * e + 5 + q // 2)
                pe.wait_ge(S["hl_done"], NQ * t + NQ + q + 1)
                terms = ((hTh, w2h), (hTl, w2h), (hTh, w2l))
                for j in range(QC):
                    for i, (hp, wp) in enumerate(terms):
                        mm = pe.matmul(scp[:, 512:512 + H], hp[:, q, j * P:(j + 1) * P], wp[:, q * QC + j, :],
                                       start=(q == 0 and j == 0 and i == 0), stop=(q == NQ - 1 and j == QC - 1 and i == 2))
                if q == NQ - 1:
                    mm.then_inc(S["y_done"], 1)

            def tile(t, e):
                gate_up(t, 0, e)
                gate_up(t, 1, e)
                turn_h(t, 0)
                gate_up(t, 2, e)
                turn_h(t, 1)
                gate_up(t, 3, e)
                turn_h(t, 2)
                down(t, 0, e)
                down(t, 1, e)
                turn_h(t, 3)
                down(t, 2, e)
                turn_x(t + 1)
                down(t, 3, e)

            pe.wait_ge(S["tiles_ready"], 1)
            turn_x(0)
            with pe.Fori(0, E) as e:
                t0 = pe.value_load(first_tile[0:1, bass.ds(e, 1)], min_val=0, max_val=TILES - 1)
                t1 = pe.value_load(first_tile[0:1, bass.ds(e + 1, 1)], min_val=1, max_val=TILES)
                with pe.Fori(t0, t1) as t:
                    tile(t, e)

        @block.scalar
        def _(act):
            act.wait_ge(S["small_in"], 16 * 7)
            act.activation(g_t[:], g_in[:], ACT.Tanh).then_inc(S["tanh_done"], 1)
            act.wait_ge(S["wkv_in"], 32)
            for w in range(2):
                act.activation(wkv[:, :, 2 * D * w:2 * D * w + D], wkv_raw[:, w], ACT.Copy).then_inc(S["wkv_hi"], 1)
            act.wait_ge(S["wsum_done"], 1)
            act.activation(wsum[:], kvp[0:2 * D, 0:H], ACT.Copy).then_inc(S["wsum_copied"], 1)

            def ctx_hi(n):
                act.wait_ge(S["ctx_turned"], n + 1)
                if n >= 2:
                    act.wait_ge(S["proj_done"], n - 1)
                region = turnB if n % 2 == 0 else turnA
                act.activation(ctxTh[n % 2][:], region[:, 0:SK], ACT.Copy).then_inc(S["ctx_hi"], 1)

            def softmax_z(b):
                act.wait_ge(S["sig_ready"], b + 1)
                act.wait_ge(S["scores_done"], b + 1)
                if b >= 1:
                    act.wait_ge(S["exp_done"], b)
                act.activation(z[:], scp[0:SQ, 0:SK], ACT.Identity, bias=sig[:, 5:6], scale=sig[:, 3:4]).then_inc(S["z_done"], 1)

            def softmax_exp(b):
                act.wait_ge(S["negmax"], b + 1)
                if b >= 1:
                    act.wait_ge(S["prob_turned"], b)
                    act.wait_ge(S["gsum"], b)
                act.activation(prob[:], z[:], ACT.Exp, bias=zmax[:, 1:2], accum_out=psum_p[:]).then_inc(S["exp_done"], 1)

            for i in ROUNDS:
                if live(i - 1):
                    softmax_z(i - 1)
                if live(i):
                    act.wait_ge(S["xn_turned"], i + 1)
                    if i >= 1:
                        act.wait_ge(S["q_done"], i)
                    act.activation(xnT[:], turnA[:, 0:HC * SQ].rearrange("p (c s) -> p c s", c=HC), ACT.Copy
                                   ).then_inc(S["xnT_copied"], 1)
                    ctx_hi(HC * i)
                    ctx_hi(HC * i + 1)
                if live(i - 1):
                    softmax_exp(i - 1)
                if live(i):
                    ctx_hi(HC * i + 2)
                    ctx_hi(HC * i + 3)
                if live(i - 1):
                    b = i - 1
                    act.wait_ge(S["prob_turned"], b + 1)
                    if b >= 1:
                        act.wait_ge(S["head_done"], b)
                    full = min(5, KT - 1)
                    act.activation(probT[:, 0:full, :], turnB[:, 0:full * SQ].rearrange("p (k s) -> p k s", k=full),
                                   ACT.Copy).then_inc(S["probT_copied"], 1)
                if live(i):
                    act.wait_ge(S["proj_done"], HC * (i + 1))
                    act.wait_ge(S["small_in"], 16 * 7)
                    if i >= 1:
                        act.wait_ge(S["scores_done"], i)
                    act.activation(kv[:], kvp[:, 0:SK], ACT.Identity, bias=kvb[:, 0:1]).then_inc(S["kv_copied"], 1)
                if live(i - 1):
                    b = i - 1
                    act.wait_ge(S["x2_ready"], b + 1)
                    act.dma_start(out[b], x2[b % 2][:]).then_inc(S[f"out_put{b % 2}"], 16)
                if live(i - 2):
                    b = i - 2
                    act.wait_ge(S["xn2_turned"], b + 1)
                    if b >= 1:
                        act.wait_ge(S["logits_done"], b)
                    act.activation(xn2T[:], turnB[:, 0:HC * SQ].rearrange("p (c s) -> p c s", c=HC), ACT.Copy
                                   ).then_inc(S["xn2T_copied"], 1)
                    act.dma_start(xn2_d[b * SQ:(b + 1) * SQ, :], xn2[b % 2][:]).then_inc(S[f"xn2_put{b % 2}"], 16)
                    act.wait_ge(S["nlmax_done"], b + 1)
                    act.wait_ge(S["logits_done"], b + 1)
                    if b >= 1:
                        act.wait_ge(S["probs_done"], b)
                    act.activation(pe_e[:], kvp[0:SQ, 768:768 + E], ACT.Exp, bias=nlmax[:], accum_out=pe_s[:, 0:1]
                                   ).then_inc(S["lexp_done"], 1)
            act.drain().then_inc(S["attn_done"], 1)

            def x_hi(t):
                act.wait_ge(S["xg_turned"], t + 1)
                act.activation(xTh[:], scp[:, 0:H].rearrange("p (c s) -> p c s", c=HC), ACT.Copy).then_inc(S["xh_done"], 1)

            def weights_hi(e, before):
                for c in range(HC):
                    act.wait_ge(S[f"st13_{c}"], 16 * e + 16)
                for q in range(NQ):
                    act.wait_ge(S["gu_done"], NQ * before + q + 1)
                    src = stage13[:].rearrange("p c (g n) -> p c g n", g=2)[:, :, :, q * QW:(q + 1) * QW]
                    dst = w13h[:].rearrange("p c (g n) -> p c g n", g=2)[:, :, :, q * QW:(q + 1) * QW]
                    act.activation(dst, src, ACT.Copy).then_inc(S["w_hi"], 1)
                for u in range(2):
                    act.wait_ge(S[f"st2_{u}"], 16 * e + 16)
                    act.wait_ge(S["y_done"], before + 1)
                    act.activation(w2h[:, u * IC // 2:(u + 1) * IC // 2, :], stage2[:, u * IC // 2:(u + 1) * IC // 2, :],
                                   ACT.Copy).then_inc(S["w_hi"], 1)

            def silu(t, q):
                act.wait_ge(S["gu_done"], NQ * t + NQ + q + 1)
                act.wait_ge(S["h_done"], NQ * t + q + 3)
                region = (turnA, turnB)[q // 2][:, (q % 2) * 512:(q % 2) * 512 + QW]
                act.activation(sg[q % 2][:], region, ACT.Silu).then_inc(S["silu_done"], 1)

            def h_hi(t, q):
                act.wait_ge(S["ht_done"], NQ * t + NQ + q + 1)
                act.wait_ge(S["y_done"], t + 1)
                act.activation(hTh[:, q, :], kvp[:, (q % 2) * 512:(q % 2) * 512 + QW], ACT.Copy).then_inc(S["hh_done"], 1)

            act.wait_ge(S["attn_done"], 4)
            act.wait_ge(S["tiles_ready"], 1)
            x_hi(0)
            with act.Fori(0, E) as e:
                t0 = act.value_load(first_tile[0:1, bass.ds(e, 1)], min_val=0, max_val=TILES - 1)
                t1 = act.value_load(first_tile[0:1, bass.ds(e + 1, 1)], min_val=1, max_val=TILES)
                weights_hi(e, t0)
                with act.Fori(t0, t1) as t:
                    silu(t, 0)
                    silu(t, 1)
                    h_hi(t, 0)
                    silu(t, 2)
                    h_hi(t, 1)
                    silu(t, 3)
                    h_hi(t, 2)
                    h_hi(t, 3)
                    x_hi(t + 1)
                    act.wait_ge(S["y_done"], t + 2)
                    act.wait_ge(S["ent_copied"], t + 1)
                    act.wait_ge(S["yw_free"], t + 1)
                    act.activation(yw[:], scp[:, 512:512 + H], ACT.Copy, scale=ent[:, 1:2].bitcast(F32)
                                   ).then_inc(S["y_ready"], 1)

        @block.vector
        def _(dve):
            dve.memset(ones[:], 1.0).then_inc(S["ones_made"], 1)
            dve.memset(kvb[:], 0.0).then_inc(S["kvb_zero"], 1)
            dve.wait_ge(S["ident_made"], 1)
            for r in range(2):
                dve.tensor_reduce(sel[:, r * D:(r + 1) * D], ident[:].rearrange("p (j m) -> p m j", m=D), AX.X, ALU.add
                                  ).then_inc(S["sel_made"], 1)
            dve.wait_ge(S["wkv_hi"], 2)
            for w in range(2):
                dve.tensor_tensor(wkv[:, :, 2 * D * w + D:2 * D * w + 2 * D], wkv_raw[:, w],
                                  wkv[:, :, 2 * D * w:2 * D * w + D].bitcast(F32), ALU.subtract).then_inc(S["wkv_lo"], 1)
            dve.wait_ge(S["small_in"], 16 * 7)
            dve.wait_ge(S["ones_made"], 1)
            dve.tensor_scalar(bv_b[:], ones[0:D, 0:SQ], bv_c[:, 0:1], None, ALU.mult).then_inc(S["bv_spread"], 1)
            dve.wait_ge(S["rw_turned"], 1)
            dve.tensor_copy(rwT[:], kvp[:, 512:512 + HC * E].rearrange("p (c e) -> p c e", c=HC)).then_inc(S["rw_copied"], 1)

            def ln1_stats(b):
                dve.wait_ge(S[f"x_in{b % 2}"], 32 * (b // 2 + 1))
                if b >= 1:
                    dve.wait_ge(S["xn_ready"], b)
                dve.bn_stats(bn1[:], x_t[b % 2][:]).then_inc(S["ln1_stat"], 1)
                dve.wait_ge(S["ln1_stat"], b + 1)
                dve.bn_aggr(ln1[:], bn1[:]).then_inc(S["ln1_aggr"], 1)

            def ctx_lo(n):
                dve.wait_ge(S["ctx_hi"], n + 1)
                region = turnB if n % 2 == 0 else turnA
                dve.tensor_tensor(ctxTl[n % 2][:], region[:, 0:SK], ctxTh[n % 2][:].bitcast(F32), ALU.subtract
                                  ).then_inc(S["ctx_lo"], 1)

            for i in ROUNDS:
                if i == -1:
                    ln1_stats(0)
                    dve.wait_ge(S["crow_done"], 1)
                    dve.wait_ge(S["tanh_done"], 1)
                    dve.tensor_scalar(crow[:], scp[0:SQ, 0:H], g_t[0:SQ, 0:1], None, ALU.mult).then_inc(S["crow_made"], 1)
                if live(i - 1):
                    b = i - 1
                    dve.wait_ge(S["scores_done"], b + 1)
                    if b >= 1:
                        dve.wait_ge(S["sig_ready"], b)
                    half_k = SK // 2
                    for j in range(2):
                        dve.bn_stats(bns[:, j, :], scp[0:SQ, j * half_k:(j + 1) * half_k]).then_inc(S["sstat0"], 1)
                    dve.wait_ge(S["sstat0"], 2 * (b + 1))
                    dve.bn_aggr(lns[:], bns[:].rearrange("p a b -> p (a b)")).then_inc(S["s_aggr"], 1)
                if live(i):
                    ctx_lo(HC * i)
                    dve.wait_ge(S["q_done"], i + 1)
                    if i >= 1:
                        dve.wait_ge(S["scores_done"], i)
                    dve.tensor_scalar(qT[:], kvp[0:2 * D, P:P + SQ], bq_c[:, 0:1], float(H) ** -0.5, ALU.add, ALU.mult
                                      ).then_inc(S["q_copied"], 1)
                    ctx_lo(HC * i + 1)
                if live(i - 1):
                    b = i - 1
                    dve.wait_ge(S["z_done"], b + 1)
                    dve.wait_ge(S["mterm_ready"], b + 1)
                    if b >= 1:
                        dve.wait_ge(S["exp_done"], b)
                    dve.tensor_tensor_reduce(out=z[:], in0=z[:], in1=mterm[b % 2][:], scale=1.0, scalar=-3.0e38,
                                             op0=ALU.add, op1=ALU.max, accum_out=zmax[:, 0:1]).then_inc(S["z_masked"], 1)
                    dve.wait_ge(S["z_masked"], b + 1)
                    dve.tensor_scalar(zmax[:, 1:2], zmax[:, 0:1], -1.0, None, ALU.mult).then_inc(S["negmax"], 1)
                if live(i):
                    ctx_lo(HC * i + 2)
                if live(i + 1) and i >= 0:
                    ln1_stats(i + 1)
                if live(i):
                    ctx_lo(HC * i + 3)
                if live(i - 1):
                    b = i - 1
                    dve.wait_ge(S["prob_turned"], b + 1)
                    if b >= 1:
                        dve.wait_ge(S["head_done"], b)
                    dve.wait_ge(S["probT_copied"], 2 * b + 1)
                    dve.tensor_copy(probT[0:KL, KT - 1, :], turnB[0:KL, 512:512 + SQ]).then_inc(S["probT_copied"], 1)
                    dve.wait_ge(S["exp_done"], b + 1)
                    if b >= 1:
                        dve.wait_ge(S["x2_ready"], b)
                    dve.reciprocal(gs[:, 0:1], psum_p[:]).then_inc(S["rsum"], 1)
                    dve.wait_ge(S["rsum"], b + 1)
                    dve.tensor_scalar(gs[:, 1:2], gs[:, 0:1], g_t[0:SQ, 0:1], None, ALU.mult).then_inc(S["gsum"], 1)
                if live(i):
                    dve.wait_ge(S["v_turned"], i + 1)
                    if i >= 2:
                        dve.wait_ge(S["head_done"], i - 1)
                    dve.tensor_copy(vn[i % 2][:, 0:KT - 1, :], turnA[:, 0:(KT - 1) * 2 * D].rearrange("p (k d) -> p k d", d=2 * D)
                                    ).then_inc(S["v_copied"], 1)
                    dve.tensor_copy(vn[i % 2][0:KL, KT - 1, :], turnA[0:KL, (KT - 1) * 2 * D:KT * 2 * D]).then_inc(S["v_copied"], 1)
                if live(i - 3):
                    b = i - 3
                    dve.wait_ge(S["lexp_done"], b + 1)
                    if b >= 1:
                        dve.wait_ge(S["weight_made"], b)
                    dve.reciprocal(pe_s[:, 1:2], pe_s[:, 0:1]).then_inc(S["lrec"], 1)
                    dve.wait_ge(S["lrec"], b + 1)
                    dve.tensor_scalar(pr[:], pe_e[:], pe_s[:, 1:2], None, ALU.mult).then_inc(S["probs_done"], 1)
                    dve.wait_ge(S["probs_done"], b + 1)
                    dve.max(ptop[:], pr[:]).then_inc(S["ptop_done"], 1)
                    dve.wait_ge(S["ptop_done"], b + 1)
                    dve.max_index(pidx[:], ptop[:], pr[:]).then_inc(S["pidx_done"], 1)
                if live(i - 1):
                    b = i - 1
                    dve.wait_ge(S["head_done"], b + 1)
                    if b >= 1:
                        dve.wait_ge(S["out_done"], b)
                    dve.tensor_copy(headT[:], kvp[0:2 * D, 0:SQ]).then_inc(S["head_copied"], 1)
                if live(i - 3):
                    b = i - 3
                    dve.wait_ge(S["rank_done"], b + 1)
                    if b >= 1:
                        dve.wait_ge(S["place_made"], b)
                    for k in range(2):
                        dve.tensor_tensor_reduce(out=hr[:, k, :], in0=kvp[0:SQ, 784:784 + E], in1=hot[b % 2][:, k, :], scale=1.0,
                                                 scalar=0.0, op0=ALU.mult, op1=ALU.add, accum_out=place_f[:, k:k + 1]
                                                 ).then_inc(S["hr_done"], 1)
                if live(i - 1):
                    b = i - 1
                    dve.wait_ge(S["out_done"], b + 1)
                    dve.wait_ge(S["gsum"], b + 1)
                    dve.wait_ge(S["xc_ready"], b + 1)
                    if b >= 2:
                        dve.wait_ge(S[f"out_put{b % 2}"], 16 * (b // 2))
                        dve.wait_ge(S["xn2_ready"], b - 1)
                    dve.scalar_tensor_tensor(out=x2[b % 2][:], in0=turnA[0:SQ, 0:H], scalar=gs[:, 1:2], in1=xc[b % 3][:],
                                             op0=ALU.mult, op1=ALU.add).then_inc(S["x2_ready"], 1)
                    dve.wait_ge(S["x2_ready"], b + 1)
                    if b >= 1:
                        dve.wait_ge(S["ln2_aggr"], b)
                    dve.bn_stats(bn2[:], x2[b % 2][:]).then_inc(S["ln2_stat"], 1)
                    dve.wait_ge(S["ln2_stat"], b + 1)
                    dve.bn_aggr(ln2[b % 2][:], bn2[:]).then_inc(S["ln2_aggr"], 1)
                if live(i - 2):
                    b = i - 2
                    dve.wait_ge(S["logits_done"], b + 1)
                    if b >= 1:
                        dve.wait_ge(S["nlmax_done"], b)
                    dve.max(ltop[:], kvp[0:SQ, 768:768 + E]).then_inc(S["lmax_done"], 1)

            dve.wait_ge(S["cnt_done"], 1)
            dve.tensor_scalar(nt[:, 0:1], kvp[0:E, 800:801], float(P - 1), None, ALU.add).then_inc(S["nt_f"], 1)
            dve.wait_ge(S["nt_f"], 1)
            dve.tensor_copy(cnt_i[:, 0:1], nt[:, 0:1]).then_inc(S["cnt_int"], 1)
            dve.wait_ge(S["cnt_int"], 1)
            dve.tensor_scalar(cnt_i[:, 1:2], cnt_i[:, 0:1], P.bit_length() - 1, None, ALU.arith_shift_right).then_inc(S["cnt_shift"], 1)
            dve.wait_ge(S["cnt_shift"], 1)
            dve.tensor_scalar(nt[:, 1:2], cnt_i[:, 1:2], 1.0, None, ALU.max).then_inc(S["nt_ready"], 1)
            dve.wait_ge(S["nt_ready"], 1)
            dve.tensor_scalar(nt[:, 2:3], nt[:, 1:2], -float(P), float(CAP), ALU.mult, ALU.add).then_inc(S["nt_f"], 1)
            dve.wait_ge(S["cum_done"], 1)
            dve.tensor_copy(ncum[:], scp[0:E, 0:1]).then_inc(S["ncum_copied"], 1)
            dve.tensor_copy(first_tile[:], scp[0:1, 512:512 + E + 1]).then_inc(S["first_ready"], 1)
            dve.wait_ge(S["ncum_copied"], 1)
            dve.wait_ge(S["nt_f"], 2)
            dve.wait_ge(S["iotas_made"], 1)
            dve.tensor_scalar(past[:], t_num[:], ncum[:, 0:1], nt[:, 2:3], ALU.is_ge, ALU.mult).then_inc(S["past_made"], 1)
            dve.wait_ge(S["tilerow_done"], 1)
            dve.scalar_tensor_tensor(out=tile_row[:], in0=t_num[0:1, :], scalar=float(P), in1=scp[0:1, 0:TILES],
                                     op0=ALU.mult, op1=ALU.add).then_inc(S["tiles_ready"], 1)
            dve.drain().then_inc(S["attn_done"], 1)

            dve.sem_inc(S["gu_done"], NQ)
            dve.sem_inc(S["h_done"], NQ)
            dve.sem_inc(S["ht_done"], NQ)
            dve.sem_inc(S["hl_done"], NQ)
            dve.sem_inc(S["y_done"], 1)
            dve.sem_inc(S["y_ready"], 1)
            dve.sem_inc(S["yw_free"], 1)

            def x_lo(t):
                dve.wait_ge(S["xh_done"], t + 1)
                dve.tensor_tensor(xTl[:], scp[:, 0:H].rearrange("p (c s) -> p c s", c=HC), xTh[:].bitcast(F32), ALU.subtract
                                  ).then_inc(S["xl_done"], 1)

            def weights_lo(e):
                for q in range(NQ):
                    dve.wait_ge(S["w_hi"], 6 * e + q + 1)
                    v = [w[:].rearrange("p c (g n) -> p c g n", g=2)[:, :, :, q * QW:(q + 1) * QW]
                         for w in (w13l, stage13, w13h)]
                    dve.tensor_tensor(v[0], v[1], v[2].bitcast(F32), ALU.subtract).then_inc(S["w_lo"], 1)
                for u in range(2):
                    dve.wait_ge(S["w_hi"], 6 * e + 5 + u)
                    v = [w[:, u * IC // 2:(u + 1) * IC // 2, :] for w in (w2l, stage2, w2h)]
                    dve.tensor_tensor(v[0], v[1], v[2].bitcast(F32), ALU.subtract).then_inc(S["w_lo"], 1)

            def h_mul(t, q):
                dve.wait_ge(S["silu_done"], NQ * t + q + 1)
                dve.wait_ge(S["ht_done"], NQ * t + q + 1)
                region = (turnA, turnB)[q // 2][:, (q % 2) * 512 + QW:(q % 2) * 512 + 2 * QW]
                dve.tensor_tensor(h_t[:, q, :], region, sg[q % 2][:], ALU.mult).then_inc(S["h_done"], 1)

            def h_lo(t, q):
                dve.wait_ge(S["hh_done"], NQ * t + q + 1)
                dve.tensor_tensor(hTl[:, q, :], kvp[:, (q % 2) * 512:(q % 2) * 512 + QW], hTh[:, q, :].bitcast(F32), ALU.subtract
                                  ).then_inc(S["hl_done"], 1)

            dve.wait_ge(S["attn_done"], 4)
            x_lo(0)
            with dve.Fori(0, E) as e:
                t0 = dve.value_load(first_tile[0:1, bass.ds(e, 1)], min_val=0, max_val=TILES - 1)
                t1 = dve.value_load(first_tile[0:1, bass.ds(e + 1, 1)], min_val=1, max_val=TILES)
                weights_lo(e)
                with dve.Fori(t0, t1) as t:
                    h_mul(t, 0)
                    h_mul(t, 1)
                    h_lo(t, 0)
                    h_mul(t, 2)
                    h_lo(t, 1)
                    h_mul(t, 3)
                    h_lo(t, 2)
                    h_lo(t, 3)
                    x_lo(t + 1)

        @block.gpsimd
        def _(pool):
            steps = [0]

            def link(ins):
                steps[0] += 1
                ins.then_inc(S["pool_w"], 1)
                pool.wait_ge(S["pool_w"], steps[0])

            link(pool.memset(ident[:], 0.0))
            pool.affine_select(out=ident[:], in_=ident[:], compare_op=ALU.not_equal, fill=1.0, base=0,
                               pattern=[[-1, P]], channel_multiplier=1).then_inc(S["ident_made"], 1)
            for n, v in enumerate((-0.5, 0.5, -1.0)):
                link(pool.memset(half[:, n:n + 1], v))

            def normalise(b, src, stats, rs, dst, done):
                link(pool.tensor_scalar(rs[:, 0:1], stats[:, 1:2], LN_EPS, None, ALU.add))
                link(pool.tensor_tensor(rs[:, 1:2], rs[:, 0:1], half[:, 0:1], ALU.pow))
                pool.tensor_scalar(dst[:], src[:], stats[:, 0:1], rs[:, 1:2], ALU.subtract, ALU.mult).then_inc(S[done], 1)

            def norm1(b):
                pool.wait_ge(S["ln1_aggr"], b + 1)
                if b >= 1:
                    pool.wait_ge(S["xn_turned"], b)
                normalise(b, x_t[b % 2], ln1, rs1, xn, "xn_ready")

            def residual(b):
                pool.wait_ge(S["crow_made"], 1)
                if b >= 3:
                    pool.wait_ge(S["x2_ready"], b - 2)
                pool.wait_ge(S[f"x_in{b % 2}"], 32 * (b // 2 + 1))
                pool.tensor_tensor(xc[b % 3][:], x_t[b % 2][:], crow[:], ALU.add).then_inc(S["xc_ready"], 1)

            def mask_term(b):
                pool.wait_ge(S[f"x_in{b % 2}"], 32 * (b // 2 + 1))
                if b >= 2:
                    pool.wait_ge(S["z_masked"], b - 1)
                pool.tensor_scalar(mterm[b % 2][:], mask_u[b % 2][:], MASK_TERM, None, ALU.mult).then_inc(S["mterm_ready"], 1)

            norm1(0)
            link(pool.memset(tri[:], 1.0))
            link(pool.affine_select(out=tri[:], in_=tri[:], compare_op=ALU.is_gt, fill=0.0, base=0,
                                    pattern=[[1, SQ]], channel_multiplier=-1))
            link(pool.memset(before8[:], 1.0))
            link(pool.affine_select(out=before8[:], in_=before8[:], compare_op=ALU.is_gt, fill=0.0, base=0,
                                    pattern=[[1, E + 1]], channel_multiplier=-1))
            link(pool.iota(tok[:], [[SQ, NB]], base=0, channel_multiplier=1))
            link(pool.iota(e_int[:], [[1, E]], base=0, channel_multiplier=0))
            link(pool.tensor_copy(e_num[:], e_int[:]))
            link(pool.tensor_scalar(e_base[:], e_num[0:1, :], float(CAP), None, ALU.mult))
            link(pool.iota(t_int[:], [[1, TILES]], base=0, channel_multiplier=0))
            pool.tensor_copy(t_num[:], t_int[:]).then_inc(S["iotas_made"], 1)
            link(pool.memset(taken[:, 0, :], 0.0))
            link(pool.memset(empty[:], 0))
            pool.memset(empty[:, :, 0:1], NO_TOKEN).then_inc(S["consts_copied"], 1)
            mask_term(0)
            residual(0)

            for i in ROUNDS:
                if i == -1:
                    continue
                if live(i - 1):
                    b = i - 1
                    pool.wait_ge(S["s_aggr"], b + 1)
                    if b >= 1:
                        pool.wait_ge(S["z_done"], b)
                    link(pool.tensor_scalar(sig[:, 0:1], lns[:, 1:2], float(SK) / (SK - 1), None, ALU.mult))
                    link(pool.tensor_tensor(sig[:, 1:2], sig[:, 0:1], half[:, 1:2], ALU.pow))
                    link(pool.tensor_scalar(sig[:, 2:3], sig[:, 1:2], SIGMA_EPS, None, ALU.add))
                    link(pool.tensor_tensor(sig[:, 3:4], sig[:, 2:3], half[:, 2:3], ALU.pow))
                    link(pool.tensor_tensor(sig[:, 4:5], lns[:, 0:1], sig[:, 3:4], ALU.mult))
                    pool.tensor_scalar(sig[:, 5:6], sig[:, 4:5], -1.0, None, ALU.mult).then_inc(S["sig_ready"], 1)
                if live(i - 2):
                    b = i - 2
                    pool.wait_ge(S["ln2_aggr"], b + 1)
                    if b >= 2:
                        pool.wait_ge(S[f"xn2_put{b % 2}"], 16 * (b // 2))
                        pool.wait_ge(S["xn2_turned"], b - 1)
                    normalise(b, x2[b % 2], ln2[b % 2], rs2, xn2[b % 2], "xn2_ready")
                if live(i + 1):
                    norm1(i + 1)
                    mask_term(i + 1)
                    residual(i + 1)
                if live(i - 3):
                    b = i - 3
                    pool.wait_ge(S["pidx_done"], b + 1)
                    if b >= 2:
                        pool.wait_ge(S["hr_done"], 2 * (b - 1))
                    link(pool.tensor_copy(idxf[:], pidx[:, 0:2]))
                    for k in range(2):
                        link(pool.tensor_scalar(hot[b % 2][:, k, :], e_num[:], idxf[:, k:k + 1], None, ALU.is_equal))
                    link(pool.tensor_tensor(both[b % 2][:], hot[b % 2][:, 0, :], hot[b % 2][:, 1, :], ALU.add))
                    pool.tensor_tensor(taken[:, b + 1, :], taken[:, b, :], both[b % 2][:], ALU.add).then_inc(S["taken_made"], 1)
                    w = wgt[b % 2]
                    link(pool.tensor_tensor(w[:, 0:1], ptop[:, 0:1], ptop[:, 1:2], ALU.add))
                    link(pool.tensor_scalar(w[:, 1:2], w[:, 0:1], TOPK_EPS, None, ALU.add))
                    link(pool.tensor_tensor(w[:, 2:3], w[:, 1:2], half[:, 2:3], ALU.pow))
                    link(pool.tensor_tensor(w[:, 3:4], w[:, 2:3], g_t[0:SQ, 1:2], ALU.mult))
                    for k in range(2):
                        link(pool.tensor_copy(entry[:, b, k, 0:1], tok[:, b:b + 1]))
                    pool.tensor_scalar(entry[:, b, :, 1].bitcast(F32), ptop[:, 0:2], w[:, 3:4], None, ALU.mult
                                       ).then_inc(S["weight_made"], 1)
                if live(i - 4) or i == NB + 3:
                    pass
                if live(i - 2):
                    b = i - 2
                    pool.wait_ge(S["lmax_done"], b + 1)
                    if b >= 1:
                        pool.wait_ge(S["lexp_done"], b)
                    pool.tensor_scalar(nlmax[:], ltop[:, 0:1], -1.0, None, ALU.mult).then_inc(S["nlmax_done"], 1)
                if live(i - 3):
                    b = i - 3
                    pool.wait_ge(S["hr_done"], 2 * (b + 1))
                    pool.tensor_copy(place[:, b, :], place_f[:]).then_inc(S["place_made"], 1)
                    pool.wait_ge(S["place_made"], b + 1)
                    pool.wait_ge(S["weight_made"], b + 1)
                    pool.wait_ge(S["lists_set"], 16)
                    if b >= 1:
                        for k in range(2):
                            pool.wait_ge(S[f"lists_put{k}"], 16 * b)
                    for k in range(2):
                        pool.indirect_dma_start(lists_d, bass.IndirectOffsetOnAxis(place[:, b, k:k + 1], 0),
                                                entry[:, b, k, :], None).then_inc(S[f"lists_put{k}"], 16)
            for k in range(2):
                pool.wait_ge(S[f"lists_put{k}"], 16 * NB)
                pool.wait_ge(S[f"xn2_put{k}"], 16 * NB // 2)
                pool.wait_ge(S[f"out_put{k}"], 16 * NB // 2)
            pool.drain().then_inc(S["attn_done"], 1)
            pool.wait_ge(S["attn_done"], 4)

            def hold(s, value):
                pool.wait_ge(s, value)
                pool.sem_inc(S["pool_held"], 1)

            def fetch(t):
                row = pool.value_load(tile_row[0:1, bass.ds(t, 1)], min_val=0, max_val=ROWS - P)
                pool.dma_start(ent_next[:], lists_d[bass.ds(row, P), :]).then_inc(S["list_in"], 16)
                hold(S["list_in"], 16 * t + 16)
                pool.tensor_scalar(gidx[:], ent_next[:, 0:1], float(T - 1), None, ALU.min).then_inc(S["gidx_made"], 1)
                hold(S["gidx_made"], t + 1)
                pool.indirect_dma_start(xg[:], None, xn2_d, bass.IndirectOffsetOnAxis(gidx[:], 0)).then_inc(S["gathered"], 16)

            pool.wait_ge(S["tiles_ready"], 1)
            fetch(0)
            n_tiles = pool.value_load(first_tile[0:1, E:E + 1], min_val=E, max_val=TILES - 1)
            with pool.Fori(0, n_tiles) as t:
                pool.tensor_copy(ent[:], ent_next[:]).then_inc(S["ent_copied"], 1)
                hold(S["ent_copied"], t + 1)
                hold(S["xg_turned"], t + 1)
                fetch(t + 1)
                hold(S["y_ready"], t + 2)
                pool.indirect_dma_start(out_rows, bass.IndirectOffsetOnAxis(ent[:, 0:1], 0), yw[:], None,
                                        bounds_check=T - 1, oob_is_err=False, compute_op=ALU.add
                                        ).then_inc(S["y_added"], 16)
                pool.wait_ge(S["y_added"], 16 * t + 16)
                pool.sem_inc(S["yw_free"], 1)


_INS = ["x", "ctx_1024", "mask_BxS2_bk0", "g_xattn", "g_ffn", "L0_xattn_Wq", "L0_xattn_bq", "L0_xattn_Wk", "L0_xattn_bk",
        "L0_xattn_Wv", "L0_xattn_bv", "L0_xattn_Wout", "L0_xattn_bout", "L0_ffn_router_w", "L0_ffn_w13", "L0_ffn_w2"]


def kernel(**inputs):
    import numpy as _np
    import concourse.bacc as _bacc
    from concourse import mybir as _mybir
    from concourse.bass_utils import run_bass_kernel_spmd as _run

    nc = _bacc.Bacc("TRN2", target_bir_lowering=False, num_devices=1)
    arrays, args = {}, []
    for name in _INS:
        a = _np.ascontiguousarray(inputs[name])
        if a.dtype == _np.bool_:
            a = a.reshape(-1).view(_np.int32)
        arrays[f"in_{name}_dram"] = a
        args.append(nc.dram_tensor(f"in_{name}_dram", a.shape, _mybir.dt.from_np(a.dtype), kind="ExternalInput").ap())
    shape = tuple(inputs["x"].shape)
    args.append(nc.dram_tensor("out_0_dram", shape, _mybir.dt.float32, kind="ExternalOutput").ap())
    gated_block(nc, *args)
    r = _run(nc, [arrays], core_ids=[0])
    return r.results[0]["out_0_dram"]
```

```python
from contextlib import ExitStack

import concourse.bass as bass
from concourse import mybir

ALU = mybir.AluOpType
ACT = mybir.ActivationFunctionType
F32 = mybir.dt.float32
F32R = mybir.dt.float32r
I32 = mybir.dt.int32
U32 = mybir.dt.uint32
U8 = mybir.dt.uint8
AX = mybir.AxisListType

P = 128
MASK_TERM = -1e-32
SIGMA_EPS = 1e-8
LN_EPS = 1e-5
TOPK_EPS = 1e-6


def gated_block(nc, x, ctx_in, mask, g_xattn, g_ffn, Wq, bq, Wk, bk, Wv, bv, Wout, bout,
                router_w, w13, w2, out):
    NB, SQ, H = x.shape
    SK = ctx_in.shape[1]
    D = Wq.shape[1]
    E, _, I2 = w13.shape
    I = I2 // 2
    HC = H // P
    IC = I // P
    T = NB * SQ
    KT = -(-SK // P)
    KL = SK - (KT - 1) * P
    REP = H // D
    CAP = -(-T // P) * P
    ROWS = E * CAP + P
    TILES = 2 * T // P + E + 1
    NQ = 4
    QW = I // NQ
    QC = QW // P
    W_UNITS = 2 * NQ + 2
    NO_TOKEN = 1 << 12
    assert NQ * 2 * QW * 4 <= 8192 and 2 * D == 64 and P % D == 0

    mask = mask.bitcast(U8).rearrange("(b k) -> b k", b=NB)

    es = ExitStack()
    with es:
        def sem(name):
            return es.enter_context(nc.semaphore(name))

        def sb(stack, name, shape, dt=F32):
            return stack.enter_context(nc.sbuf_tensor(name, shape, dt))

        mterm_d = nc.dram_tensor("mterm_d", [NB, SK], F32).ap()
        xn2_d = nc.dram_tensor("xn2_d", [T, H], F32).ap()
        lists_d = nc.dram_tensor("lists_d", [ROWS, 2], I32).ap()
        out_rows = out.rearrange("b s d -> (b s) d")

        turnA = es.enter_context(nc.psum_tensor("turnA", [P, 1024], F32))
        turnB = es.enter_context(nc.psum_tensor("turnB", [P, 1024], F32))
        kvp = es.enter_context(nc.psum_tensor("kvp", [P, 1024], F32))
        scp = es.enter_context(nc.psum_tensor("scp", [P, 1024], F32))

        ident = sb(es, "ident", [P, P])
        ones = sb(es, "ones", [P, P])
        stage13 = sb(es, "stage13", [P, HC, I2])
        stage2 = sb(es, "stage2", [P, IC, H])
        w13h = sb(es, "w13h", [P, HC, I2], F32R)
        w13l = sb(es, "w13l", [P, HC, I2], F32R)
        first_tile = sb(es, "first_tile", [1, E + 1], I32)
        last_tile = sb(es, "last_tile", [1, E + 1], I32)
        tile_row = sb(es, "tile_row", [1, TILES], I32)

        a = ExitStack()
        ctx_t = [sb(a, f"ctx_t{i}", [P, KT, H]) for i in range(2)]
        x_t = [sb(a, f"x_t{i}", [SQ, H]) for i in range(2)]
        mask_u = sb(a, "mask_u", [NB, SK], U8)
        mask_f = sb(a, "mask_f", [NB, SK])
        mterm = [sb(a, f"mterm{i}", [SQ, SK]) for i in range(2)]
        ctxTh = [sb(a, f"ctxTh{i}", [P, SK], F32R) for i in range(2)]
        ctxTl = [sb(a, f"ctxTl{i}", [P, SK], F32R) for i in range(2)]
        kv = sb(a, "kv", [P, SK])
        z = sb(a, "z", [SQ, SK])
        prob = sb(a, "prob", [SQ, SK])
        probT = sb(a, "probT", [P, KT, SQ])
        vn = [sb(a, f"vn{i}", [P, KT, 2 * D]) for i in range(2)]
        xn = sb(a, "xn", [SQ, H])
        xnT = sb(a, "xnT", [P, HC, SQ])
        qT = sb(a, "qT", [2 * D, SQ])
        headT = sb(a, "headT", [2 * D, SQ])
        xc = [sb(a, f"xc{i}", [SQ, H]) for i in range(3)]
        x2 = [sb(a, f"x2{i}", [SQ, H]) for i in range(2)]
        xn2 = [sb(a, f"xn2{i}", [SQ, H]) for i in range(2)]
        xn2T = sb(a, "xn2T", [P, HC, SQ])
        wq2 = sb(a, "wq2", [P, HC, 2 * D])
        wkv_raw = sb(a, "wkv_raw", [P, 2, HC, D])
        wkv = sb(a, "wkv", [P, HC, P], F32R)
        wsum = sb(a, "wsum", [2 * D, H])
        sel = sb(a, "sel", [P, 2 * D])
        rw_rows = xc[1][0:E, :]
        rwT = sb(a, "rwT", [P, HC, E])
        bout_r = xc[2][0:1, :]
        bv_c = sb(a, "bv_c", [D, 1])
        bv_b = sb(a, "bv_b", [D, SQ])
        bq_c = sb(a, "bq_c", [2 * D, 1])
        kvb = sb(a, "kvb", [P, 1])
        g_in = sb(a, "g_in", [P, 2])
        g_t = sb(a, "g_t", [P, 2])
        crow = sb(a, "crow", [SQ, H])
        tri = sb(a, "tri", [SQ, SQ])
        before8 = sb(a, "before8", [E, E + 1])
        tok = sb(a, "tok", [SQ, NB], I32)
        e_int = sb(a, "e_int", [SQ, E], I32)
        e_num = sb(a, "e_num", [SQ, E])
        e_base = sb(a, "e_base", [1, E])
        t_int = sb(a, "t_int", [E, TILES], I32)
        t_num = sb(a, "t_num", [E, TILES])
        empty = sb(a, "empty", [P, ROWS // P, 2], I32)
        half = sb(a, "half", [SQ, 3])
        bn1 = sb(a, "bn1", [SQ, 6])
        ln1 = sb(a, "ln1", [SQ, 2])
        rs1 = sb(a, "rs1", [SQ, 2])
        bns = sb(a, "bns", [SQ, 2, 6])
        lns = sb(a, "lns", [SQ, 2])
        sig = sb(a, "sig", [SQ, 6])
        zmax = sb(a, "zmax", [SQ, 2])
        psum_p = sb(a, "psum_p", [SQ, 1])
        gs = sb(a, "gs", [SQ, 2])
        bn2 = sb(a, "bn2", [SQ, 6])
        ln2 = [sb(a, f"ln2{i}", [SQ, 2]) for i in range(2)]
        rs2 = sb(a, "rs2", [SQ, 2])
        logits = sb(a, "logits", [SQ, E])
        ltop = sb(a, "ltop", [SQ, 8])
        nlmax = sb(a, "nlmax", [SQ, 1])
        pe_e = sb(a, "pe_e", [SQ, E])
        pe_s = sb(a, "pe_s", [SQ, 2])
        pr = sb(a, "pr", [SQ, E])
        ptop = sb(a, "ptop", [SQ, 8])
        pidx = sb(a, "pidx", [SQ, 8], U32)
        idxf = sb(a, "idxf", [SQ, 2])
        hot = [sb(a, f"hot{i}", [SQ, 2, E]) for i in range(2)]
        both = [sb(a, f"both{i}", [SQ, E]) for i in range(2)]
        taken = sb(a, "taken", [SQ, NB + 1, E])
        wgt = [sb(a, f"wgt{i}", [SQ, 4]) for i in range(2)]
        hr = sb(a, "hr", [SQ, 2, E])
        place_f = sb(a, "place_f", [SQ, 2])
        place = sb(a, "place", [SQ, NB, 2], I32)
        entry = sb(a, "entry", [SQ, NB, 2, 2], I32)
        cnt_i = sb(a, "cnt_i", [E, 2], I32)
        nt = sb(a, "nt", [E, 3])
        past = sb(a, "past", [E, TILES])
        ncum = sb(a, "ncum", [E, 1])
        a.close()

        w2h = sb(es, "w2h", [P, IC, H], F32R)
        w2l = sb(es, "w2l", [P, IC, H], F32R)
        xg = sb(es, "xg", [P, H])
        xTh = sb(es, "xTh", [P, HC, P], F32R)
        xTl = sb(es, "xTl", [P, HC, P], F32R)
        sg = [sb(es, f"sg{i}", [P, QW]) for i in range(2)]
        h_t = sb(es, "h_t", [P, NQ, QW])
        hTh = sb(es, "hTh", [P, NQ, QC * P], F32R)
        hTl = sb(es, "hTl", [P, NQ, QC * P], F32R)
        yw = sb(es, "yw", [P, H])
        ent_next = sb(es, "ent_next", [P, 2], I32)
        ent_now = sb(es, "ent_now", [P, 2], I32)
        ent = sb(es, "ent", [P, 2], I32)
        gidx = sb(es, "gidx", [P, 1], I32)

        names = """x_in0 x_in1 ctx_in0 ctx_in1 wout_in wq_in wkv_in small_in rw_in lists_set lists_put0 lists_put1
        out_put0 out_put1 xn2_put0 xn2_put1
        ident_made ones_made iotas_made consts_copied kvb_zero
        sel_made wsum_done wsum_copied wkv_hi wkv_lo rw_turned rw_copied tanh_done bv_spread crow_done crow_made
        ln1_stat ln1_aggr rstd1 xn_ready xc_ready mterm_in0 mterm_in1 mterm_put mask_in mask_made
        xn_turned xnT_copied q_done q_copied ctx_turned ctx_hi ctx_lo proj_done kv_copied
        v_turned v_copied scores_done sstat0 s_aggr sig_ready z_done z_masked negmax exp_done rsum
        gsum prob_turned probT_copied head_done head_copied out_done x2_ready ln2_stat ln2_aggr rstd2
        xn2_ready xn2_turned xn2T_copied logits_done logits_copied lmax_done nlmax_done lexp_done lrec probs_done ptop_done pidx_done
        pool_w pool_held taken_made weight_made rank_done hr_done place_made
        cnt_done cnt_int cnt_shift nt_f nt_ready cum_done ncum_copied past_made tilerow_done tiles_ready first_ready
        attn_done""".split()
        S = {n: sem(n) for n in names}
        names2 = """st13_0 st13_1 st13_2 st13_3 st2_0 st2_1
        w_hi w_lo gu_done silu_done h_done ht_done hh_done hl_done y_done y_ready
        list_in gidx_made gathered yw_free ent_kept ent_copied y_added xg_turned xh_done xl_done""".split()
        S.update({n: sem(n) for n in names2})

        block = es.enter_context(nc.Block())
        ROUNDS = range(-1, NB + 4)

        def live(b):
            return 0 <= b < NB

        def early_units(i):
            start = {NB: 0, NB + 1: 2, NB + 2: 5, NB + 3: 2 * NQ}
            return range(start[i], start[i + 1]) if i in start and i + 1 in start else range(0)

        def unit_of(weights, unit):
            gate_up, down = weights
            if unit < 2 * NQ:
                q, r = unit // 2, unit % 2
                rows = slice(r * HC // 2, (r + 1) * HC // 2)
                return gate_up[:].rearrange("p c (g n) -> p c g n", g=2)[:, rows, :, q * QW:(q + 1) * QW]
            u = unit - 2 * NQ
            return down[:, u * IC // 2:(u + 1) * IC // 2, :]

        def tiles_of(eng, e):
            t0 = eng.value_load(first_tile[0:1, bass.ds(e, 1)], min_val=0, max_val=TILES - 1)
            t1 = eng.value_load(first_tile[0:1, bass.ds(e + 1, 1)], min_val=1, max_val=TILES)
            return t0, t1

        def all_but_last(eng, t0, last, tile):
            with eng.If_lt(eng.to_reg(t0), eng.to_reg(last)):
                with eng.Fori(t0, last) as t:
                    tile(t)

        @block.sync
        def _(sp):
            sp.dma_start(x_t[0][:], x[0]).then_inc(S["x_in0"], 16)
            sp.dma_start(mask_u[:], mask).then_inc(S["mask_in"], 16)
            sp.dma_start(ctx_t[1][:, 0:HC, :], Wout.rearrange("(c p) n -> p c n", p=P)).then_inc(S["wout_in"], 16)
            sp.dma_start(wkv_raw[:, 0], Wk.rearrange("(c p) n -> p c n", p=P)).then_inc(S["wkv_in"], 16)
            sp.dma_start(wkv_raw[:, 1], Wv.rearrange("(c p) n -> p c n", p=P)).then_inc(S["wkv_in"], 16)
            for r in range(2):
                sp.dma_start(wq2[:, :, r * D:(r + 1) * D], Wq.rearrange("(c p) n -> p c n", p=P)).then_inc(S["wq_in"], 16)

            def load_ctx(b):
                s = S[f"ctx_in{b % 2}"]
                sp.dma_start(ctx_t[b % 2][:, 0:KT - 1, :],
                             ctx_in[b, 0:(KT - 1) * P, :].rearrange("(k p) d -> p k d", p=P)).then_inc(s, 16)
                sp.dma_start(ctx_t[b % 2][0:KL, KT - 1, :], ctx_in[b, (KT - 1) * P:SK, :]).then_inc(s, 16)

            load_ctx(0)
            sp.dma_start(rw_rows, router_w).then_inc(S["rw_in"], 16)
            sp.wait_ge(S["kvb_zero"], 1)
            sp.dma_start(kvb[0:D, :], bk.rearrange("(d o) -> d o", o=1)).then_inc(S["small_in"], 16)
            sp.dma_start(bv_c[:], bv.rearrange("(d o) -> d o", o=1)).then_inc(S["small_in"], 16)
            for r in range(2):
                sp.dma_start(bq_c[r * D:(r + 1) * D, :], bq.rearrange("(d o) -> d o", o=1)).then_inc(S["small_in"], 16)
            sp.dma_start(bout_r, bout.rearrange("(o d) -> o d", o=1)).then_inc(S["small_in"], 16)
            sp.dma_start(g_in[:, 0:1], g_xattn.rearrange("(o d) -> o d", o=1).partition_broadcast(P)).then_inc(S["small_in"], 16)
            sp.dma_start(g_in[:, 1:2], g_ffn.rearrange("(o d) -> o d", o=1).partition_broadcast(P)).then_inc(S["small_in"], 16)
            def load_mterm(b):
                if b == 0:
                    sp.wait_ge(S["mterm_put"], 16)
                if b >= 2:
                    sp.wait_ge(S["z_masked"], b - 1)
                sp.dma_start(mterm[b % 2][:], mterm_d[b:b + 1, :].partition_broadcast(SQ)).then_inc(S[f"mterm_in{b % 2}"], 16)

            for b in range(1, NB):
                s = S[f"x_in{b % 2}"]
                if b >= 2:
                    sp.wait_ge(S["xn_ready"], b - 1)
                    sp.wait_ge(S["xc_ready"], b - 1)
                sp.dma_start(x_t[b % 2][:], x[b]).then_inc(s, 16)
                load_mterm(b - 1)
                if b == 1:
                    sp.wait_ge(S["wsum_done"], 1)
                else:
                    sp.wait_ge(S["ctx_turned"], HC * (b - 1))
                load_ctx(b)
                if b == 2:
                    sp.wait_ge(S["consts_copied"], 1)
                    sp.dma_start(lists_d.rearrange("(p r) t -> p r t", p=P), empty[:]).then_inc(S["lists_set"], 16)

            load_mterm(NB - 1)

            def load_w13(e, c):
                sp.dma_start(stage13[:, c, :], w13[e, c * P:(c + 1) * P, :]).then_inc(S[f"st13_{c}"], 16)

            def load_w2(e, u):
                half_ic = IC // 2
                sp.dma_start(stage2[:, u * half_ic:(u + 1) * half_ic, :],
                             w2[e, u * half_ic * P:(u + 1) * half_ic * P, :].rearrange("(c p) n -> p c n", p=P)
                             ).then_inc(S[f"st2_{u}"], 16)

            for c in range(HC):
                load_w13(0, c)
            for u in range(2):
                load_w2(0, u)
            sp.wait_ge(S["attn_done"], 4)
            with sp.Fori(1, E) as e:
                sp.wait_ge(S["w_lo"], e * W_UNITS - 2)
                before = sp.value_load(first_tile[0:1, bass.ds(e - 1, 1)], min_val=0, max_val=TILES - 1)
                sp.wait_ge(S["gathered"], before * 16 + 32)
                for c in range(HC):
                    sp.dma_start(stage13[:, c, :], w13[bass.ds(e, 1), c * P:(c + 1) * P, :].rearrange("o p n -> p (o n)")
                                 ).then_inc(S[f"st13_{c}"], 16)
                for u in range(2):
                    sp.wait_ge(S["w_lo"], e * W_UNITS - 1 + u)
                    hic = IC // 2
                    sp.dma_start(stage2[:, u * hic:(u + 1) * hic, :],
                                 w2[bass.ds(e, 1), u * hic * P:(u + 1) * hic * P, :].rearrange("o (c p) n -> p (o c) n", p=P)
                                 ).then_inc(S[f"st2_{u}"], 16)

        @block.tensor
        def _(pe):
            pe.wait_ge(S["ident_made"], 1)
            pe.wait_ge(S["ones_made"], 1)
            pe.wait_ge(S["wout_in"], 16)
            pe.wait_ge(S["sel_made"], 2)
            for c in range(HC):
                mm = pe.matmul(kvp[0:2 * D, 0:H], sel[:], ctx_t[1][:, c, :], start=(c == 0), stop=(c == HC - 1))
            mm.then_inc(S["wsum_done"], 1)
            pe.wait_ge(S["rw_in"], 16)
            for c in range(HC):
                mm = pe.transpose(kvp[:, 512 + E * c:512 + E * (c + 1)], rw_rows[:, c * P:(c + 1) * P], ident[0:E, 0:E])
            mm.then_inc(S["rw_turned"], 1)
            pe.wait_ge(S["wsum_copied"], 1)
            pe.wait_ge(S["bv_spread"], 1)
            pe.wait_ge(S["small_in"], 16 * 7)
            pe.matmul(scp[0:SQ, 0:H], bv_b[:], wsum[0:D, :], start=True, stop=False)
            pe.matmul(scp[0:SQ, 0:H], ones[0:1, 0:SQ], bout_r, start=False, stop=True).then_inc(S["crow_done"], 1)
            pe.wait_ge(S["rw_copied"], 1)

            def turn_ctx(b, c):
                region = turnB if c % 2 == 0 else turnA
                for k in range(KT):
                    n = P if k < KT - 1 else KL
                    mm = pe.transpose(region[:, k * P:k * P + n], ctx_t[b % 2][0:n, k, c * P:(c + 1) * P], ident[0:n, 0:n])
                mm.then_inc(S["ctx_turned"], 1)

            def project(b, c):
                n = HC * b + c
                pe.wait_ge(S["ctx_lo"], n + 1)
                for i, part in enumerate((ctxTh[n % 2], ctxTl[n % 2])):
                    for k0, k1 in ((0, 512), (512, SK)):
                        mm = pe.matmul(kvp[:, k0:k1], wkv[:, c, :], part[:, k0:k1], start=(c == 0 and i == 0),
                                       stop=(c == HC - 1 and i == 1))
                mm.then_inc(S["proj_done"], 1)

            for i in ROUNDS:
                if live(i):
                    pe.wait_ge(S["xn_ready"], i + 1)
                    if i >= 1:
                        pe.wait_ge(S["ctx_lo"], HC * i)
                    if i >= 3:
                        pe.wait_ge(S["xn2T_copied"], i - 2)
                    for c in range(HC):
                        mm = pe.transpose(turnA[:, 512 + c * SQ:512 + (c + 1) * SQ], xn[:, c * P:(c + 1) * P], ident[0:SQ, 0:SQ])
                    mm.then_inc(S["xn_turned"], 1)
                    pe.wait_ge(S[f"ctx_in{i % 2}"], 32 * (i // 2 + 1))
                    if i >= 2:
                        pe.wait_ge(S["probT_copied"], 2 * (i - 1))
                    turn_ctx(i, 0)
                    pe.wait_ge(S["xnT_copied"], i + 1)
                    if i == 0:
                        pe.wait_ge(S["wq_in"], 32)
                        pe.wait_ge(S["wkv_lo"], 2)
                    if i >= 1:
                        pe.wait_ge(S["kv_copied"], i)
                    if i >= 2:
                        pe.wait_ge(S["head_copied"], i - 1)
                    for c in range(HC):
                        mm = pe.matmul(kvp[0:2 * D, P:P + SQ], wq2[:, c, :], xnT[:, c, :], start=(c == 0), stop=(c == HC - 1))
                    mm.then_inc(S["q_done"], 1)
                if live(i - 3):
                    b = i - 3
                    pe.wait_ge(S["xn2T_copied"], b + 1)
                    if b >= 1:
                        pe.wait_ge(S["hr_done"], 2 * b)
                    for c in range(HC):
                        mm = pe.matmul(kvp[0:SQ, 768:768 + E], xn2T[:, c, :], rwT[:, c, :], start=(c == 0), stop=(c == HC - 1))
                    mm.then_inc(S["logits_done"], 1)
                if live(i):
                    if i >= 2:
                        pe.wait_ge(S["x2_ready"], i - 1)
                    elif i == 1:
                        pe.wait_ge(S["v_copied"], 2)
                    turn_ctx(i, 1)
                    pe.wait_ge(S["q_copied"], i + 1)
                    if i >= 3:
                        pe.wait_ge(S["logits_copied"], i - 2)
                    project(i, 0)
                    turn_ctx(i, 2)
                    project(i, 1)
                    turn_ctx(i, 3)
                    project(i, 2)
                    project(i, 3)
                if live(i - 1):
                    b = i - 1
                    pe.wait_ge(S["exp_done"], b + 1)
                    for k in range(KT):
                        n = P if k < KT - 1 else KL
                        mm = pe.transpose(turnB[0:n, (k // 5) * 512 + (k % 5) * SQ:(k // 5) * 512 + (k % 5) * SQ + SQ],
                                          prob[:, k * P:k * P + n], ident[0:SQ, 0:SQ])
                    mm.then_inc(S["prob_turned"], 1)
                if live(i - 2):
                    b = i - 2
                    pe.wait_ge(S["xn2_ready"], b + 1)
                    for c in range(HC):
                        mm = pe.transpose(turnA[:, 512 + c * SQ:512 + (c + 1) * SQ], xn2[b % 2][:, c * P:(c + 1) * P], ident[0:SQ, 0:SQ])
                    mm.then_inc(S["xn2_turned"], 1)
                if live(i):
                    pe.wait_ge(S["kv_copied"], i + 1)
                    for k in range(KT):
                        n = P if k < KT - 1 else KL
                        mm = pe.transpose(turnA[0:n, k * 2 * D:(k + 1) * 2 * D], kv[2 * D:4 * D, k * P:k * P + n],
                                          ident[2 * D:4 * D, 2 * D:4 * D])
                    mm.then_inc(S["v_turned"], 1)
                    if i == 0:
                        pe.wait_ge(S["crow_made"], 1)
                    if i >= 1:
                        pe.wait_ge(S["z_done"], i)
                    for k0, k1 in ((0, 512), (512, SK)):
                        mm = pe.matmul(scp[0:SQ, k0:k1], qT[:], kv[0:2 * D, k0:k1], start=True, stop=True)
                    mm.then_inc(S["scores_done"], 1)
                if live(i - 1):
                    b = i - 1
                    pe.wait_ge(S["probT_copied"], 2 * (b + 1))
                    pe.wait_ge(S["v_copied"], 2 * (b + 1))
                    for k in range(KT):
                        n = P if k < KT - 1 else KL
                        mm = pe.matmul(kvp[0:2 * D, 0:SQ], vn[b % 2][0:n, k, :], probT[0:n, k, :], start=(k == 0), stop=(k == KT - 1))
                    mm.then_inc(S["head_done"], 1)
                if live(i - 3):
                    b = i - 3
                    pe.wait_ge(S["taken_made"], b + 1)
                    pe.wait_ge(S["logits_copied"], b + 1)
                    pe.matmul(kvp[0:SQ, 784:784 + E], tri[:], both[b % 2][:], start=True, stop=False)
                    pe.matmul(kvp[0:SQ, 784:784 + E], ones[0:SQ, 0:SQ], taken[:, b, :], start=False, stop=False)
                    pe.matmul(kvp[0:SQ, 784:784 + E], ones[0:1, 0:SQ], e_base[:], start=False, stop=True).then_inc(S["rank_done"], 1)
                if live(i - 1):
                    b = i - 1
                    pe.wait_ge(S["head_copied"], b + 1)
                    if live(i):
                        pe.wait_ge(S["v_copied"], 2 * (i + 1))
                    pe.matmul(turnA[0:SQ, 0:H], headT[:], wsum[:], start=True, stop=True).then_inc(S["out_done"], 1)

            pe.wait_ge(S["hr_done"], 2 * NB)
            pe.matmul(kvp[0:E, 800:801], taken[:, NB, :], ones[0:SQ, 0:1], start=True, stop=True).then_inc(S["cnt_done"], 1)
            pe.wait_ge(S["nt_ready"], 1)
            pe.matmul(scp[0:E, 0:1], before8[:, 1:E + 1], nt[:, 1:2], start=True, stop=True)
            pe.matmul(scp[0:1, 512:512 + E + 1], nt[:, 1:2], before8[:], start=True, stop=True).then_inc(S["cum_done"], 1)
            pe.wait_ge(S["past_made"], 1)
            pe.wait_ge(S["first_ready"], 2)
            pe.matmul(scp[0:1, 0:TILES], ones[0:E - 1, 0:1], past[0:E - 1, :], start=True, stop=True).then_inc(S["tilerow_done"], 1)
            pe.drain().then_inc(S["attn_done"], 1)

            def turn_x(t):
                pe.wait_ge(S["gathered"], 16 * t + 16)
                for c in range(HC):
                    mm = pe.transpose(scp[:, c * P:(c + 1) * P], xg[:, c * P:(c + 1) * P], ident[:])
                mm.then_inc(S["xg_turned"], 1)

            def gate_up(t, q, e):
                if q == 0:
                    pe.wait_ge(S["xl_done"], t + 1)
                pe.wait_ge(S["h_done"], NQ * t + q + 1)
                region = (turnA, turnB)[q // 2][:, (q % 2) * 512:(q % 2) * 512 + 2 * QW]
                terms = ((xTh, w13h), (xTl, w13h), (xTh, w13l))
                for c in range(HC):
                    if c % (HC // 2) == 0:
                        pe.wait_ge(S["w_lo"], e * W_UNITS + 2 * q + c // (HC // 2) + 1)
                    for i, (xp, wp) in enumerate(terms):
                        rhs = wp[:, c, :].rearrange("p (g n) -> p g n", g=2)[:, :, q * QW:(q + 1) * QW]
                        mm = pe.matmul(region, xp[:, c, :], rhs, start=(c == 0 and i == 0), stop=(c == HC - 1 and i == 2))
                mm.then_inc(S["gu_done"], 1)

            def turn_h(t, q):
                pe.wait_ge(S["h_done"], NQ * t + NQ + q + 1)
                pe.wait_ge(S["hl_done"], NQ * t + q + 3)
                for j in range(QC):
                    mm = pe.transpose(kvp[:, (q % 2) * 512 + j * P:(q % 2) * 512 + (j + 1) * P],
                                      h_t[:, q, j * P:(j + 1) * P], ident[:])
                mm.then_inc(S["ht_done"], 1)

            def down(t, q, e):
                if q == 0:
                    pe.wait_ge(S["y_ready"], t + 1)
                if q % 2 == 0:
                    pe.wait_ge(S["w_lo"], e * W_UNITS + 2 * NQ + 1 + q // 2)
                pe.wait_ge(S["hl_done"], NQ * t + NQ + q + 1)
                terms = ((hTh, w2h), (hTl, w2h), (hTh, w2l))
                for j in range(QC):
                    for i, (hp, wp) in enumerate(terms):
                        mm = pe.matmul(scp[:, 512:512 + H], hp[:, q, j * P:(j + 1) * P], wp[:, q * QC + j, :],
                                       start=(q == 0 and j == 0 and i == 0), stop=(q == NQ - 1 and j == QC - 1 and i == 2))
                if q == NQ - 1:
                    mm.then_inc(S["y_done"], 1)

            def tile(t, e):
                gate_up(t, 0, e)
                gate_up(t, 1, e)
                gate_up(t, 2, e)
                turn_h(t, 0)
                gate_up(t, 3, e)
                turn_h(t, 1)
                down(t, 0, e)
                turn_h(t, 2)
                down(t, 1, e)
                turn_h(t, 3)
                down(t, 2, e)
                turn_x(t + 1)
                down(t, 3, e)

            pe.wait_ge(S["tiles_ready"], 1)
            turn_x(0)
            with pe.Fori(0, E) as e:
                t0, t1 = tiles_of(pe, e)
                with pe.Fori(t0, t1) as t:
                    tile(t, e)

        @block.scalar
        def _(act):
            act.wait_ge(S["small_in"], 16 * 7)
            act.activation(g_t[:], g_in[:], ACT.Tanh).then_inc(S["tanh_done"], 1)
            act.wait_ge(S["wkv_in"], 32)
            for w in range(2):
                act.activation(wkv[:, :, 2 * D * w:2 * D * w + D], wkv_raw[:, w], ACT.Copy).then_inc(S["wkv_hi"], 1)
            act.wait_ge(S["wsum_done"], 1)
            act.activation(wsum[:], kvp[0:2 * D, 0:H], ACT.Copy).then_inc(S["wsum_copied"], 1)

            def ctx_hi(n):
                act.wait_ge(S["ctx_turned"], n + 1)
                if n >= 2:
                    act.wait_ge(S["proj_done"], n - 1)
                region = turnB if n % 2 == 0 else turnA
                act.activation(ctxTh[n % 2][:], region[:, 0:SK], ACT.Copy).then_inc(S["ctx_hi"], 1)

            def softmax_z(b):
                act.wait_ge(S["sig_ready"], b + 1)
                act.wait_ge(S["scores_done"], b + 1)
                if b >= 1:
                    act.wait_ge(S["exp_done"], b)
                act.activation(z[:], scp[0:SQ, 0:SK], ACT.Identity, bias=sig[:, 5:6], scale=sig[:, 3:4]).then_inc(S["z_done"], 1)

            def softmax_exp(b):
                act.wait_ge(S["negmax"], b + 1)
                if b >= 1:
                    act.wait_ge(S["prob_turned"], b)
                    act.wait_ge(S["gsum"], b)
                act.activation(prob[:], z[:], ACT.Exp, bias=zmax[:, 1:2], accum_out=psum_p[:]).then_inc(S["exp_done"], 1)

            def split_hi(e, unit, last):
                if unit == 0:
                    for c in range(HC):
                        act.wait_ge(S[f"st13_{c}"], e * 16 + 16)
                if unit >= 2 * NQ:
                    act.wait_ge(S[f"st2_{unit - 2 * NQ}"], e * 16 + 16)
                if last is not None:
                    if unit < 2 * NQ:
                        act.wait_ge(S["gu_done"], NQ * last + NQ + unit // 2 + 1)
                    else:
                        act.wait_ge(S["y_done"], last + 2)
                dst, src = unit_of((w13h, w2h), unit), unit_of((stage13, stage2), unit)
                act.activation(dst, src, ACT.Copy).then_inc(S["w_hi"], 1)

            for i in ROUNDS:
                if live(i):
                    act.wait_ge(S["xn_turned"], i + 1)
                    if i >= 1:
                        act.wait_ge(S["q_done"], i)
                    act.activation(xnT[:], turnA[:, 512:512 + HC * SQ].rearrange("p (c s) -> p c s", c=HC), ACT.Copy
                                   ).then_inc(S["xnT_copied"], 1)
                    ctx_hi(HC * i)
                if live(i - 1):
                    softmax_z(i - 1)
                if live(i):
                    ctx_hi(HC * i + 1)
                if live(i - 2):
                    b = i - 2
                    act.wait_ge(S["x2_ready"], b + 1)
                    act.dma_start(out[b], x2[b % 2][:]).then_inc(S[f"out_put{b % 2}"], 16)
                if live(i - 3):
                    b = i - 3
                    act.wait_ge(S["nlmax_done"], b + 1)
                    if b >= 1:
                        act.wait_ge(S["probs_done"], b)
                    act.activation(pe_e[:], logits[:], ACT.Exp, bias=nlmax[:], accum_out=pe_s[:, 0:1]
                                   ).then_inc(S["lexp_done"], 1)
                if live(i):
                    ctx_hi(HC * i + 2)
                if live(i - 1):
                    softmax_exp(i - 1)
                for unit in early_units(i):
                    if i == NB:
                        split_hi(0, unit, None)
                if live(i):
                    ctx_hi(HC * i + 3)
                    act.wait_ge(S["proj_done"], HC * (i + 1))
                    act.wait_ge(S["small_in"], 16 * 7)
                    if i >= 1:
                        act.wait_ge(S["scores_done"], i)
                    act.activation(kv[:], kvp[:, 0:SK], ACT.Identity, bias=kvb[:, 0:1]).then_inc(S["kv_copied"], 1)
                if live(i - 1):
                    b = i - 1
                    act.wait_ge(S["prob_turned"], b + 1)
                    if b >= 1:
                        act.wait_ge(S["head_done"], b)
                    full = min(5, KT - 1)
                    act.activation(probT[:, 0:full, :], turnB[:, 0:full * SQ].rearrange("p (k s) -> p k s", k=full),
                                   ACT.Copy).then_inc(S["probT_copied"], 1)
                if live(i - 2):
                    b = i - 2
                    act.wait_ge(S["xn2_turned"], b + 1)
                    if b >= 1:
                        act.wait_ge(S["logits_done"], b)
                    act.activation(xn2T[:], turnA[:, 512:512 + HC * SQ].rearrange("p (c s) -> p c s", c=HC), ACT.Copy
                                   ).then_inc(S["xn2T_copied"], 1)
                    act.dma_start(xn2_d[b * SQ:(b + 1) * SQ, :], xn2[b % 2][:]).then_inc(S[f"xn2_put{b % 2}"], 16)
                for unit in early_units(i):
                    if i > NB:
                        split_hi(0, unit, None)
            act.drain().then_inc(S["attn_done"], 1)

            def x_hi(t):
                act.wait_ge(S["xg_turned"], t + 1)
                act.activation(xTh[:], scp[:, 0:H].rearrange("p (c s) -> p c s", c=HC), ACT.Copy).then_inc(S["xh_done"], 1)

            def silu(t, q):
                act.wait_ge(S["gu_done"], NQ * t + NQ + q + 1)
                act.wait_ge(S["h_done"], NQ * t + q + 3)
                region = (turnA, turnB)[q // 2][:, (q % 2) * 512:(q % 2) * 512 + QW]
                act.activation(sg[q % 2][:], region, ACT.Silu).then_inc(S["silu_done"], 1)

            def h_hi(t, q):
                act.wait_ge(S["ht_done"], NQ * t + NQ + q + 1)
                act.wait_ge(S["y_done"], t + 1)
                act.activation(hTh[:, q, :], kvp[:, (q % 2) * 512:(q % 2) * 512 + QW], ACT.Copy).then_inc(S["hh_done"], 1)

            act.wait_ge(S["attn_done"], 4)
            act.wait_ge(S["tiles_ready"], 1)
            act.activation(sg[0][:, 0:1], ident[:, 0:1], ACT.Silu)

            def y_out(t):
                act.wait_ge(S["y_done"], t + 2)
                act.wait_ge(S["ent_copied"], t + 1)
                act.wait_ge(S["yw_free"], t + 1)
                act.activation(yw[:], scp[:, 512:512 + H], ACT.Copy, scale=ent[:, 1:2].bitcast(F32)
                               ).then_inc(S["y_ready"], 1)

            def tile(t, e_next):
                def split(*units):
                    if e_next is not None:
                        for unit in units:
                            split_hi(e_next, unit, t)

                silu(t, 0)
                split(0, 1)
                silu(t, 1)
                split(2, 3)
                silu(t, 2)
                h_hi(t, 0)
                split(4, 5)
                silu(t, 3)
                h_hi(t, 1)
                split(6)
                h_hi(t, 2)
                split(7)
                h_hi(t, 3)
                x_hi(t + 1)
                y_out(t)
                split(8, 9)

            for unit in (8, 9):
                split_hi(0, unit, None)
            x_hi(0)
            with act.Fori(0, E - 1) as e:
                t0, t1 = tiles_of(act, e)
                last = act.value_load(last_tile[0:1, bass.ds(e + 1, 1)], min_val=0, max_val=TILES - 1)
                all_but_last(act, t0, last, lambda t: tile(t, None))
                tile(last, e + 1)
            t0, t1 = tiles_of(act, E - 1)
            with act.Fori(t0, t1) as t:
                tile(t, None)

        @block.vector
        def _(dve):
            dve.memset(ones[:], 1.0).then_inc(S["ones_made"], 1)
            dve.memset(kvb[:], 0.0).then_inc(S["kvb_zero"], 1)
            dve.wait_ge(S["ident_made"], 1)
            for r in range(2):
                dve.tensor_reduce(sel[:, r * D:(r + 1) * D], ident[:].rearrange("p (j m) -> p m j", m=D), AX.X, ALU.add
                                  ).then_inc(S["sel_made"], 1)
            dve.wait_ge(S["wkv_hi"], 2)
            for w in range(2):
                dve.tensor_tensor(wkv[:, :, 2 * D * w + D:2 * D * w + 2 * D], wkv_raw[:, w],
                                  wkv[:, :, 2 * D * w:2 * D * w + D].bitcast(F32), ALU.subtract).then_inc(S["wkv_lo"], 1)
            dve.wait_ge(S["small_in"], 16 * 7)
            dve.wait_ge(S["ones_made"], 1)
            dve.tensor_scalar(bv_b[:], ones[0:D, 0:SQ], bv_c[:, 0:1], None, ALU.mult).then_inc(S["bv_spread"], 1)
            dve.wait_ge(S["rw_turned"], 1)
            dve.tensor_copy(rwT[:], kvp[:, 512:512 + HC * E].rearrange("p (c e) -> p c e", c=HC)).then_inc(S["rw_copied"], 1)

            def ln1_stats(b):
                dve.wait_ge(S[f"x_in{b % 2}"], 16 * (b // 2 + 1))
                if b >= 1:
                    dve.wait_ge(S["xn_ready"], b)
                dve.bn_stats(bn1[:], x_t[b % 2][:]).then_inc(S["ln1_stat"], 1)
                dve.wait_ge(S["ln1_stat"], b + 1)
                dve.bn_aggr(ln1[:], bn1[:]).then_inc(S["ln1_aggr"], 1)

            def normalise(src, stats, rs, dst, done):
                dve.tensor_scalar(dst[:], src[:], stats[:, 0:1], rs[:, 1:2], ALU.subtract, ALU.mult).then_inc(S[done], 1)

            def normalise1(b):
                dve.wait_ge(S["rstd1"], b + 1)
                if b >= 1:
                    dve.wait_ge(S["xn_turned"], b)
                normalise(x_t[b % 2], ln1, rs1, xn, "xn_ready")

            def ctx_lo(n):
                dve.wait_ge(S["ctx_hi"], n + 1)
                region = turnB if n % 2 == 0 else turnA
                dve.tensor_tensor(ctxTl[n % 2][:], region[:, 0:SK], ctxTh[n % 2][:].bitcast(F32), ALU.subtract
                                  ).then_inc(S["ctx_lo"], 1)

            def split_lo(e, unit):
                dve.wait_ge(S["w_hi"], e * W_UNITS + unit + 1)
                lo, raw, hi = (unit_of(w, unit) for w in ((w13l, w2l), (stage13, stage2), (w13h, w2h)))
                dve.tensor_tensor(lo, raw, hi.bitcast(F32), ALU.subtract).then_inc(S["w_lo"], 1)

            for i in ROUNDS:
                if i == -1:
                    ln1_stats(0)
                    normalise1(0)
                    dve.wait_ge(S["crow_done"], 1)
                    dve.wait_ge(S["tanh_done"], 1)
                    dve.tensor_scalar(crow[:], scp[0:SQ, 0:H], g_t[0:SQ, 0:1], None, ALU.mult).then_inc(S["crow_made"], 1)
                if live(i):
                    ctx_lo(HC * i)
                    dve.wait_ge(S["q_done"], i + 1)
                    if i >= 1:
                        dve.wait_ge(S["scores_done"], i)
                    dve.tensor_scalar(qT[:], kvp[0:2 * D, P:P + SQ], bq_c[:, 0:1], float(H) ** -0.5, ALU.add, ALU.mult
                                      ).then_inc(S["q_copied"], 1)
                if live(i - 3):
                    b = i - 3
                    dve.wait_ge(S["logits_done"], b + 1)
                    if b >= 1:
                        dve.wait_ge(S["lexp_done"], b)
                    dve.tensor_copy(logits[:], kvp[0:SQ, 768:768 + E]).then_inc(S["logits_copied"], 1)
                    dve.wait_ge(S["logits_copied"], b + 1)
                    dve.max(ltop[:], logits[:]).then_inc(S["lmax_done"], 1)
                if live(i - 2):
                    b = i - 2
                    dve.wait_ge(S["rstd2"], b + 1)
                    if b >= 2:
                        dve.wait_ge(S[f"xn2_put{b % 2}"], 16 * (b // 2))
                        dve.wait_ge(S["xn2_turned"], b - 1)
                    normalise(x2[b % 2], ln2[b % 2], rs2, xn2[b % 2], "xn2_ready")
                if live(i):
                    ctx_lo(HC * i + 1)
                if live(i - 1):
                    b = i - 1
                    dve.wait_ge(S["z_done"], b + 1)
                    dve.wait_ge(S[f"mterm_in{b % 2}"], 16 * (b // 2 + 1))
                    if b >= 1:
                        dve.wait_ge(S["exp_done"], b)
                    dve.tensor_tensor_reduce(out=z[:], in0=z[:], in1=mterm[b % 2][:], scale=1.0, scalar=-3.0e38,
                                             op0=ALU.add, op1=ALU.max, accum_out=zmax[:, 0:1]).then_inc(S["z_masked"], 1)
                    dve.wait_ge(S["z_masked"], b + 1)
                    dve.tensor_scalar(zmax[:, 1:2], zmax[:, 0:1], -1.0, None, ALU.mult).then_inc(S["negmax"], 1)
                if live(i):
                    ctx_lo(HC * i + 2)
                if live(i - 3):
                    b = i - 3
                    dve.wait_ge(S["lexp_done"], b + 1)
                    if b >= 1:
                        dve.wait_ge(S["weight_made"], b)
                    dve.reciprocal(pe_s[:, 1:2], pe_s[:, 0:1]).then_inc(S["lrec"], 1)
                    dve.wait_ge(S["lrec"], b + 1)
                    dve.tensor_scalar(pr[:], pe_e[:], pe_s[:, 1:2], None, ALU.mult).then_inc(S["probs_done"], 1)
                    dve.wait_ge(S["probs_done"], b + 1)
                    dve.max(ptop[:], pr[:]).then_inc(S["ptop_done"], 1)
                    dve.wait_ge(S["ptop_done"], b + 1)
                    dve.max_index(pidx[:], ptop[:], pr[:]).then_inc(S["pidx_done"], 1)
                for unit in early_units(i):
                    split_lo(0, unit)
                if live(i + 1) and i >= 0:
                    ln1_stats(i + 1)
                if live(i):
                    ctx_lo(HC * i + 3)
                if live(i + 1) and i >= 0:
                    normalise1(i + 1)
                if live(i - 1):
                    b = i - 1
                    dve.wait_ge(S["exp_done"], b + 1)
                    if b >= 1:
                        dve.wait_ge(S["x2_ready"], b)
                    dve.reciprocal(gs[:, 0:1], psum_p[:]).then_inc(S["rsum"], 1)
                    dve.wait_ge(S["rsum"], b + 1)
                    dve.tensor_scalar(gs[:, 1:2], gs[:, 0:1], g_t[0:SQ, 0:1], None, ALU.mult).then_inc(S["gsum"], 1)
                    dve.wait_ge(S["prob_turned"], b + 1)
                    if b >= 1:
                        dve.wait_ge(S["head_done"], b)
                    dve.tensor_copy(probT[0:KL, KT - 1, :], turnB[0:KL, 512:512 + SQ]).then_inc(S["probT_copied"], 1)
                if live(i):
                    dve.wait_ge(S["v_turned"], i + 1)
                    if i >= 2:
                        dve.wait_ge(S["head_done"], i - 1)
                    dve.tensor_copy(vn[i % 2][:, 0:KT - 1, :], turnA[:, 0:(KT - 1) * 2 * D].rearrange("p (k d) -> p k d", d=2 * D)
                                    ).then_inc(S["v_copied"], 1)
                    dve.tensor_copy(vn[i % 2][0:KL, KT - 1, :], turnA[0:KL, (KT - 1) * 2 * D:KT * 2 * D]).then_inc(S["v_copied"], 1)
                if live(i - 1):
                    b = i - 1
                    dve.wait_ge(S["head_done"], b + 1)
                    if b >= 1:
                        dve.wait_ge(S["out_done"], b)
                    dve.tensor_copy(headT[:], kvp[0:2 * D, 0:SQ]).then_inc(S["head_copied"], 1)
                if live(i):
                    dve.wait_ge(S["scores_done"], i + 1)
                    if i >= 1:
                        dve.wait_ge(S["sig_ready"], i)
                    half_k = SK // 2
                    for j in range(2):
                        dve.bn_stats(bns[:, j, :], scp[0:SQ, j * half_k:(j + 1) * half_k]).then_inc(S["sstat0"], 1)
                    dve.wait_ge(S["sstat0"], 2 * (i + 1))
                    dve.bn_aggr(lns[:], bns[:].rearrange("p a b -> p (a b)")).then_inc(S["s_aggr"], 1)
                if live(i - 3):
                    b = i - 3
                    dve.wait_ge(S["rank_done"], b + 1)
                    if b >= 1:
                        dve.wait_ge(S["place_made"], b)
                    for k in range(2):
                        dve.tensor_tensor_reduce(out=hr[:, k, :], in0=kvp[0:SQ, 784:784 + E], in1=hot[b % 2][:, k, :], scale=1.0,
                                                 scalar=0.0, op0=ALU.mult, op1=ALU.add, accum_out=place_f[:, k:k + 1]
                                                 ).then_inc(S["hr_done"], 1)
                if live(i - 1):
                    b = i - 1
                    dve.wait_ge(S["out_done"], b + 1)
                    dve.wait_ge(S["gsum"], b + 1)
                    dve.wait_ge(S["xc_ready"], b + 1)
                    if b >= 2:
                        dve.wait_ge(S[f"out_put{b % 2}"], 16 * (b // 2))
                        dve.wait_ge(S["xn2_ready"], b - 1)
                    dve.scalar_tensor_tensor(out=x2[b % 2][:], in0=turnA[0:SQ, 0:H], scalar=gs[:, 1:2], in1=xc[b % 3][:],
                                             op0=ALU.mult, op1=ALU.add).then_inc(S["x2_ready"], 1)
                    dve.wait_ge(S["x2_ready"], b + 1)
                    if b >= 1:
                        dve.wait_ge(S["ln2_aggr"], b)
                    dve.bn_stats(bn2[:], x2[b % 2][:]).then_inc(S["ln2_stat"], 1)
                    dve.wait_ge(S["ln2_stat"], b + 1)
                    dve.bn_aggr(ln2[b % 2][:], bn2[:]).then_inc(S["ln2_aggr"], 1)

            dve.wait_ge(S["cnt_done"], 1)
            dve.tensor_scalar(nt[:, 0:1], kvp[0:E, 800:801], float(P - 1), None, ALU.add).then_inc(S["nt_f"], 1)
            dve.wait_ge(S["nt_f"], 1)
            dve.tensor_copy(cnt_i[:, 0:1], nt[:, 0:1]).then_inc(S["cnt_int"], 1)
            dve.wait_ge(S["cnt_int"], 1)
            dve.tensor_scalar(cnt_i[:, 1:2], cnt_i[:, 0:1], P.bit_length() - 1, None, ALU.arith_shift_right).then_inc(S["cnt_shift"], 1)
            dve.wait_ge(S["cnt_shift"], 1)
            dve.tensor_scalar(nt[:, 1:2], cnt_i[:, 1:2], 1.0, None, ALU.max).then_inc(S["nt_ready"], 1)
            dve.wait_ge(S["nt_ready"], 1)
            dve.tensor_scalar(nt[:, 2:3], nt[:, 1:2], -float(P), float(CAP), ALU.mult, ALU.add).then_inc(S["nt_f"], 1)
            dve.wait_ge(S["cum_done"], 1)
            dve.tensor_copy(ncum[:], scp[0:E, 0:1]).then_inc(S["ncum_copied"], 1)
            dve.tensor_copy(first_tile[:], scp[0:1, 512:512 + E + 1]).then_inc(S["first_ready"], 1)
            dve.tensor_scalar(last_tile[:], scp[0:1, 512:512 + E + 1], -1.0, None, ALU.add).then_inc(S["first_ready"], 1)
            dve.wait_ge(S["ncum_copied"], 1)
            dve.wait_ge(S["nt_f"], 2)
            dve.wait_ge(S["iotas_made"], 1)
            dve.tensor_scalar(past[:], t_num[:], ncum[:, 0:1], nt[:, 2:3], ALU.is_ge, ALU.mult).then_inc(S["past_made"], 1)
            dve.wait_ge(S["tilerow_done"], 1)
            dve.scalar_tensor_tensor(out=tile_row[:], in0=t_num[0:1, :], scalar=float(P), in1=scp[0:1, 0:TILES],
                                     op0=ALU.mult, op1=ALU.add).then_inc(S["tiles_ready"], 1)
            dve.drain().then_inc(S["attn_done"], 1)

            dve.sem_inc(S["gu_done"], NQ)
            dve.sem_inc(S["h_done"], NQ)
            dve.sem_inc(S["ht_done"], NQ)
            dve.sem_inc(S["hl_done"], NQ)
            dve.sem_inc(S["y_done"], 1)
            dve.sem_inc(S["y_ready"], 1)
            dve.sem_inc(S["yw_free"], 1)

            def x_lo(t):
                dve.wait_ge(S["xh_done"], t + 1)
                dve.tensor_tensor(xTl[:], scp[:, 0:H].rearrange("p (c s) -> p c s", c=HC), xTh[:].bitcast(F32), ALU.subtract
                                  ).then_inc(S["xl_done"], 1)

            def h_mul(t, q):
                dve.wait_ge(S["silu_done"], NQ * t + q + 1)
                dve.wait_ge(S["ht_done"], NQ * t + q + 1)
                region = (turnA, turnB)[q // 2][:, (q % 2) * 512 + QW:(q % 2) * 512 + 2 * QW]
                dve.tensor_tensor(h_t[:, q, :], region, sg[q % 2][:], ALU.mult).then_inc(S["h_done"], 1)

            def h_lo(t, q):
                dve.wait_ge(S["hh_done"], NQ * t + q + 1)
                dve.tensor_tensor(hTl[:, q, :], kvp[:, (q % 2) * 512:(q % 2) * 512 + QW], hTh[:, q, :].bitcast(F32), ALU.subtract
                                  ).then_inc(S["hl_done"], 1)

            dve.wait_ge(S["attn_done"], 4)

            def tile(t, e_next):
                def split(*units):
                    if e_next is not None:
                        for unit in units:
                            split_lo(e_next, unit)

                h_mul(t, 0)
                split(0, 1)
                h_mul(t, 1)
                split(2, 3)
                h_mul(t, 2)
                h_lo(t, 0)
                split(4)
                h_mul(t, 3)
                h_lo(t, 1)
                split(5)
                h_lo(t, 2)
                split(6)
                h_lo(t, 3)
                split(7)
                x_lo(t + 1)
                split(8, 9)

            for unit in (8, 9):
                split_lo(0, unit)
            x_lo(0)
            with dve.Fori(0, E - 1) as e:
                t0, t1 = tiles_of(dve, e)
                last = dve.value_load(last_tile[0:1, bass.ds(e + 1, 1)], min_val=0, max_val=TILES - 1)
                all_but_last(dve, t0, last, lambda t: tile(t, None))
                tile(last, e + 1)
            t0, t1 = tiles_of(dve, E - 1)
            with dve.Fori(t0, t1) as t:
                tile(t, None)

        @block.gpsimd
        def _(pool):
            steps = [0]

            def link(ins):
                steps[0] += 1
                ins.then_inc(S["pool_w"], 1)
                pool.wait_ge(S["pool_w"], steps[0])

            link(pool.memset(ident[:], 0.0))
            pool.affine_select(out=ident[:], in_=ident[:], compare_op=ALU.not_equal, fill=1.0, base=0,
                               pattern=[[-1, P]], channel_multiplier=1).then_inc(S["ident_made"], 1)
            for n, v in enumerate((-0.5, 0.5, -1.0)):
                link(pool.memset(half[:, n:n + 1], v))

            def rstd(stats, rs, done):
                link(pool.tensor_scalar(rs[:, 0:1], stats[:, 1:2], LN_EPS, None, ALU.add))
                pool.tensor_tensor(rs[:, 1:2], rs[:, 0:1], half[:, 0:1], ALU.pow).then_inc(S[done], 1)

            def norm1(b):
                pool.wait_ge(S["ln1_aggr"], b + 1)
                if b >= 1:
                    pool.wait_ge(S["xn_ready"], b)
                rstd(ln1, rs1, "rstd1")

            def residual(b):
                pool.wait_ge(S["crow_made"], 1)
                if b >= 3:
                    pool.wait_ge(S["x2_ready"], b - 2)
                pool.wait_ge(S[f"x_in{b % 2}"], 16 * (b // 2 + 1))
                pool.tensor_tensor(xc[b % 3][:], x_t[b % 2][:], crow[:], ALU.add).then_inc(S["xc_ready"], 1)

            pool.wait_ge(S["mask_in"], 16)
            pool.tensor_scalar(mask_f[:], mask_u[:], MASK_TERM, None, ALU.mult).then_inc(S["mask_made"], 1)
            pool.wait_ge(S["mask_made"], 1)
            pool.dma_start(mterm_d, mask_f[:]).then_inc(S["mterm_put"], 16)
            norm1(0)
            link(pool.memset(tri[:], 1.0))
            link(pool.affine_select(out=tri[:], in_=tri[:], compare_op=ALU.is_gt, fill=0.0, base=0,
                                    pattern=[[1, SQ]], channel_multiplier=-1))
            link(pool.memset(before8[:], 1.0))
            link(pool.affine_select(out=before8[:], in_=before8[:], compare_op=ALU.is_gt, fill=0.0, base=0,
                                    pattern=[[1, E + 1]], channel_multiplier=-1))
            link(pool.iota(tok[:], [[SQ, NB]], base=0, channel_multiplier=1))
            link(pool.iota(e_int[:], [[1, E]], base=0, channel_multiplier=0))
            link(pool.tensor_copy(e_num[:], e_int[:]))
            link(pool.tensor_scalar(e_base[:], e_num[0:1, :], float(CAP), None, ALU.mult))
            link(pool.iota(t_int[:], [[1, TILES]], base=0, channel_multiplier=0))
            pool.tensor_copy(t_num[:], t_int[:]).then_inc(S["iotas_made"], 1)
            link(pool.memset(taken[:, 0, :], 0.0))
            link(pool.memset(empty[:], 0))
            pool.memset(empty[:, :, 0:1], NO_TOKEN).then_inc(S["consts_copied"], 1)
            residual(0)

            def scatter(b):
                pool.wait_ge(S["hr_done"], 2 * (b + 1))
                pool.tensor_copy(place[:, b, :], place_f[:]).then_inc(S["place_made"], 1)
                pool.wait_ge(S["place_made"], b + 1)
                pool.wait_ge(S["weight_made"], b + 1)
                pool.wait_ge(S["lists_set"], 16)
                for k in range(2):
                    if b >= 1:
                        pool.wait_ge(S[f"lists_put{k}"], 16 * b)
                    pool.indirect_dma_start(lists_d, bass.IndirectOffsetOnAxis(place[:, b, k:k + 1], 0),
                                            entry[:, b, k, :], None).then_inc(S[f"lists_put{k}"], 16)

            for i in ROUNDS:
                if live(i - 2):
                    b = i - 2
                    pool.wait_ge(S["ln2_aggr"], b + 1)
                    if b >= 1:
                        pool.wait_ge(S["xn2_ready"], b)
                    rstd(ln2[b % 2], rs2, "rstd2")
                if live(i - 3):
                    b = i - 3
                    pool.wait_ge(S["lmax_done"], b + 1)
                    if b >= 1:
                        pool.wait_ge(S["lexp_done"], b)
                    pool.tensor_scalar(nlmax[:], ltop[:, 0:1], -1.0, None, ALU.mult).then_inc(S["nlmax_done"], 1)
                if live(i - 4):
                    scatter(i - 4)
                if live(i + 1) and i >= 0:
                    residual(i + 1)
                if live(i - 3):
                    b = i - 3
                    pool.wait_ge(S["pidx_done"], b + 1)
                    if b >= 2:
                        pool.wait_ge(S["hr_done"], 2 * (b - 1))
                        pool.wait_ge(S["rank_done"], b - 1)
                    link(pool.tensor_copy(idxf[:], pidx[:, 0:2]))
                    for k in range(2):
                        link(pool.tensor_scalar(hot[b % 2][:, k, :], e_num[:], idxf[:, k:k + 1], None, ALU.is_equal))
                    link(pool.tensor_tensor(both[b % 2][:], hot[b % 2][:, 0, :], hot[b % 2][:, 1, :], ALU.add))
                    pool.tensor_tensor(taken[:, b + 1, :], taken[:, b, :], both[b % 2][:], ALU.add).then_inc(S["taken_made"], 1)
                if live(i + 1) and i >= 0:
                    norm1(i + 1)
                if live(i - 3):
                    b = i - 3
                    w = wgt[b % 2]
                    link(pool.tensor_tensor(w[:, 0:1], ptop[:, 0:1], ptop[:, 1:2], ALU.add))
                    link(pool.tensor_scalar(w[:, 1:2], w[:, 0:1], TOPK_EPS, None, ALU.add))
                    link(pool.tensor_tensor(w[:, 2:3], w[:, 1:2], half[:, 2:3], ALU.pow))
                    link(pool.tensor_tensor(w[:, 3:4], w[:, 2:3], g_t[0:SQ, 1:2], ALU.mult))
                    for k in range(2):
                        link(pool.tensor_copy(entry[:, b, k, 0:1], tok[:, b:b + 1]))
                    pool.tensor_scalar(entry[:, b, :, 1].bitcast(F32), ptop[:, 0:2], w[:, 3:4], None, ALU.mult
                                       ).then_inc(S["weight_made"], 1)
                if live(i):
                    pool.wait_ge(S["s_aggr"], i + 1)
                    if i >= 1:
                        pool.wait_ge(S["z_done"], i)
                    link(pool.tensor_scalar(sig[:, 0:1], lns[:, 1:2], float(SK) / (SK - 1), None, ALU.mult))
                    link(pool.tensor_tensor(sig[:, 1:2], sig[:, 0:1], half[:, 1:2], ALU.pow))
                    link(pool.tensor_scalar(sig[:, 2:3], sig[:, 1:2], SIGMA_EPS, None, ALU.add))
                    link(pool.tensor_tensor(sig[:, 3:4], sig[:, 2:3], half[:, 2:3], ALU.pow))
                    link(pool.tensor_tensor(sig[:, 4:5], lns[:, 0:1], sig[:, 3:4], ALU.mult))
                    pool.tensor_scalar(sig[:, 5:6], sig[:, 4:5], -1.0, None, ALU.mult).then_inc(S["sig_ready"], 1)
            for k in range(2):
                pool.wait_ge(S[f"lists_put{k}"], 16 * NB)
                pool.wait_ge(S[f"xn2_put{k}"], 16 * NB // 2)
                pool.wait_ge(S[f"out_put{k}"], 16 * NB // 2)
            pool.drain().then_inc(S["attn_done"], 1)
            pool.wait_ge(S["attn_done"], 4)

            def hold(s, value):
                pool.wait_ge(s, value)
                pool.sem_inc(S["pool_held"], 1)

            def fetch(t):
                row = pool.value_load(tile_row[0:1, bass.ds(t, 1)], min_val=0, max_val=ROWS - P)
                pool.dma_start(ent_next[:], lists_d[bass.ds(row, P), :]).then_inc(S["list_in"], 16)
                hold(S["list_in"], 16 * t + 16)
                pool.tensor_scalar(gidx[:], ent_next[:, 0:1], float(T - 1), None, ALU.min).then_inc(S["gidx_made"], 1)
                hold(S["gidx_made"], t + 1)
                pool.indirect_dma_start(xg[:], None, xn2_d, bass.IndirectOffsetOnAxis(gidx[:], 0)).then_inc(S["gathered"], 16)

            def entries_stay(t):
                pool.tensor_copy(ent_now[:], ent_next[:]).then_inc(S["ent_kept"], 1)
                hold(S["ent_kept"], t + 1)

            def entries_pass(t):
                pool.tensor_copy(ent[:], ent_now[:]).then_inc(S["ent_copied"], 1)
                hold(S["ent_copied"], t + 1)

            def add_rows(t):
                hold(S["y_ready"], t + 2)
                pool.indirect_dma_start(out_rows, bass.IndirectOffsetOnAxis(ent[:, 0:1], 0), yw[:], None,
                                        bounds_check=T - 1, oob_is_err=False, compute_op=ALU.add
                                        ).then_inc(S["y_added"], 16)
                pool.wait_ge(S["y_added"], 16 * t + 16)
                pool.sem_inc(S["yw_free"], 1)

            pool.wait_ge(S["tiles_ready"], 1)
            fetch(0)
            entries_stay(0)
            hold(S["xg_turned"], 1)
            fetch(1)
            entries_pass(0)
            n_tiles = pool.value_load(first_tile[0:1, E:E + 1], min_val=E, max_val=TILES - 1)
            with pool.Fori(1, n_tiles) as t:
                entries_stay(t)
                hold(S["xg_turned"], t + 1)
                fetch(t + 1)
                add_rows(t - 1)
                entries_pass(t)
            add_rows(n_tiles - 1)


_INS = ["x", "ctx_1024", "mask_BxS2_bk0", "g_xattn", "g_ffn", "L0_xattn_Wq", "L0_xattn_bq", "L0_xattn_Wk", "L0_xattn_bk",
        "L0_xattn_Wv", "L0_xattn_bv", "L0_xattn_Wout", "L0_xattn_bout", "L0_ffn_router_w", "L0_ffn_w13", "L0_ffn_w2"]


def kernel(**inputs):
    import numpy as _np
    import concourse.bacc as _bacc
    from concourse import mybir as _mybir
    from concourse.bass_utils import run_bass_kernel_spmd as _run

    nc = _bacc.Bacc("TRN2", target_bir_lowering=False, num_devices=1)
    arrays, args = {}, []
    for name in _INS:
        a = _np.ascontiguousarray(inputs[name])
        if a.dtype == _np.bool_:
            a = a.reshape(-1).view(_np.int32)
        arrays[f"in_{name}_dram"] = a
        args.append(nc.dram_tensor(f"in_{name}_dram", a.shape, _mybir.dt.from_np(a.dtype), kind="ExternalInput").ap())
    shape = tuple(inputs["x"].shape)
    args.append(nc.dram_tensor("out_0_dram", shape, _mybir.dt.float32, kind="ExternalOutput").ap())
    gated_block(nc, *args)
    r = _run(nc, [arrays], core_ids=[0])
    return r.results[0]["out_0_dram"]
```
